# Optimizing a Trainium2 kernel written in Bass

```python
import numpy as np
import jax
import jax.numpy as jnp

def _softmax(x, axis=-1):
    return jax.nn.softmax(x, axis=axis)

def _gelu(x):
    return jax.nn.gelu(x, approximate=True)

def _silu(x):
    return jax.nn.silu(x)

def _sigmoid(x):
    return jax.nn.sigmoid(x)

def _layernorm(x, axis=-1, eps=1e-05):
    m = jnp.mean(x, axis=axis, keepdims=True)
    v = jnp.var(x, axis=axis, keepdims=True)
    return (x - m) / jnp.sqrt(v + eps)

def _scatter_add(tgt, idx, src, axis=0):
    return tgt.at[idx].add(src)

def _segment_sum(src, seg, n):
    return jax.ops.segment_sum(src, seg, n)
kernel_name = 'mk_macaron_d1_jaxref_r8_a0e4fb'

def setup_inputs(seed: int=0):
    np.random.seed(seed)
    _w = jnp.asarray

    def _L0_attn_setup():
        import jax, jax.numpy as jnp
        import numpy as np
        HEADS = 16

        def _fm(t):
            return jax.nn.elu(t) + 1.0
        key = jax.random.key(seed)
        ks = jax.random.split(key, 9)
        B, N, D = (4, 1024, 128)
        s = 1.0 / np.sqrt(D)
        return {'x': jax.random.normal(ks[0], (B, N, D), dtype=jnp.float32), 'wq': jax.random.normal(ks[1], (D, D), dtype=jnp.float32) * s, 'bq': jnp.zeros((D,), dtype=jnp.float32), 'wk': jax.random.normal(ks[2], (D, D), dtype=jnp.float32) * s, 'bk': jnp.zeros((D,), dtype=jnp.float32), 'wv': jax.random.normal(ks[3], (D, D), dtype=jnp.float32) * s, 'bv': jnp.zeros((D,), dtype=jnp.float32), 'wo': jax.random.normal(ks[4], (D, D), dtype=jnp.float32) * s, 'bo': jnp.zeros((D,), dtype=jnp.float32)}
    _L0_attn_in = _L0_attn_setup()

    def _L0_ffn_setup():
        import jax, jax.numpy as jnp
        import numpy as np
        DIM = 128

        def _reference_tuple_inner(x, W_r, W_k, W_v, mu_r, mu_k):
            B, T, C = x.shape
            x_prev = jnp.concatenate([jnp.zeros((B, 1, C), x.dtype), x[:, :-1, :]], axis=1)
            xr = mu_r * x + (1.0 - mu_r) * x_prev
            xk = mu_k * x + (1.0 - mu_k) * x_prev
            r = jax.nn.sigmoid(jnp.einsum('btc,dc->btd', xr, W_r))
            k = jnp.einsum('btc,dc->btd', xk, W_k)
            k_act = jnp.square(jax.nn.relu(k))
            out = r * jnp.einsum('btc,dc->btd', k_act, W_v)
            new_state = x[:, -1, :]
            return (out, new_state)
        key = jax.random.key(seed)
        ks = jax.random.split(key, 6)
        B, T, C = (8, 256, DIM)
        x = jax.random.normal(ks[0], (B, T, C), dtype=jnp.float32)
        s = 1.0 / np.sqrt(C)
        W_r = jax.random.uniform(ks[1], (C, C), jnp.float32, -s, s)
        W_k = jax.random.uniform(ks[2], (C, C), jnp.float32, -s, s)
        W_v = jax.random.uniform(ks[3], (C, C), jnp.float32, -s, s)
        mu_r = jax.random.uniform(ks[4], (C,), jnp.float32)
        mu_k = jax.random.uniform(ks[5], (C,), jnp.float32)
        return {'x': x, 'W_r': W_r, 'W_k': W_k, 'W_v': W_v, 'mu_r': mu_r, 'mu_k': mu_k}
    _L0_ffn_in = _L0_ffn_setup()
    _d = {'L0_attn_x': _L0_attn_in['x'], 'L0_attn_wq': _L0_attn_in['wq'], 'L0_attn_bq': _L0_attn_in['bq'], 'L0_attn_wk': _L0_attn_in['wk'], 'L0_attn_bk': _L0_attn_in['bk'], 'L0_attn_wv': _L0_attn_in['wv'], 'L0_attn_bv': _L0_attn_in['bv'], 'L0_attn_wo': _L0_attn_in['wo'], 'L0_attn_bo': _L0_attn_in['bo'], 'L0_ffn_W_r': _L0_ffn_in['W_r'], 'L0_ffn_W_k': _L0_ffn_in['W_k'], 'L0_ffn_W_v': _L0_ffn_in['W_v'], 'L0_ffn_mu_r': _L0_ffn_in['mu_r'], 'L0_ffn_mu_k': _L0_ffn_in['mu_k']}
    _x0 = _d['L0_attn_x']
    _d['L0_attn_x'] = jax.random.normal(jax.random.fold_in(jax.random.key(seed), 1), (8, 512, 128), dtype=_x0.dtype)
    del _x0
    return _d

def reference(L0_attn_x, L0_attn_wq, L0_attn_bq, L0_attn_wk, L0_attn_bk, L0_attn_wv, L0_attn_bv, L0_attn_wo, L0_attn_bo, L0_ffn_W_r, L0_ffn_W_k, L0_ffn_W_v, L0_ffn_mu_r, L0_ffn_mu_k):

    def _L0_attn_ref(x, wq, bq, wk, bk, wv, bv, wo, bo):
        import jax, jax.numpy as jnp
        import numpy as np
        HEADS = 16

        def _fm(t):
            return jax.nn.elu(t) + 1.0
        B, N, D = x.shape
        H = HEADS
        Dh = D // H
        q = _fm((x @ wq + bq).reshape(B, N, H, Dh))
        k = _fm((x @ wk + bk).reshape(B, N, H, Dh))
        v = (x @ wv + bv).reshape(B, N, H, Dh)
        kv = jnp.einsum('bnhd,bnhe->bhde', k, v)
        z = 1.0 / (jnp.einsum('bnhd,bhd->bnh', q, k.sum(axis=1)) + 1e-06)
        scores = jnp.einsum('bnhd,bhde,bnh->bnhe', q, kv, z)
        out = scores.reshape(B, N, D) @ wo + bo
        return out

    def _L0_ffn_ref(x, W_r, W_k, W_v, mu_r, mu_k):
        import jax, jax.numpy as jnp
        import numpy as np
        DIM = 128

        def _reference_tuple_inner(x, W_r, W_k, W_v, mu_r, mu_k):
            B, T, C = x.shape
            x_prev = jnp.concatenate([jnp.zeros((B, 1, C), x.dtype), x[:, :-1, :]], axis=1)
            xr = mu_r * x + (1.0 - mu_r) * x_prev
            xk = mu_k * x + (1.0 - mu_k) * x_prev
            r = jax.nn.sigmoid(jnp.einsum('btc,dc->btd', xr, W_r))
            k = jnp.einsum('btc,dc->btd', xk, W_k)
            k_act = jnp.square(jax.nn.relu(k))
            out = r * jnp.einsum('btc,dc->btd', k_act, W_v)
            new_state = x[:, -1, :]
            return (out, new_state)
        return _reference_tuple_inner(x, W_r, W_k, W_v, mu_r, mu_k)[0]
    x = L0_attn_x
    x = x + 0.5 * _L0_ffn_ref(_layernorm(x, axis=-1), L0_ffn_W_r, L0_ffn_W_k, L0_ffn_W_v, L0_ffn_mu_r, L0_ffn_mu_k)
    x = x + _L0_attn_ref(_layernorm(x, axis=-1), L0_attn_wq, L0_attn_bq, L0_attn_wk, L0_attn_bk, L0_attn_wv, L0_attn_bv, L0_attn_wo, L0_attn_bo)
    x = x + 0.5 * _L0_ffn_ref(_layernorm(x, axis=-1), L0_ffn_W_r, L0_ffn_W_k, L0_ffn_W_v, L0_ffn_mu_r, L0_ffn_mu_k)
    return x

_drawn_inputs = setup_inputs


def setup_inputs(seed=0):
    import zlib

    import numpy as np

    out = dict(_drawn_inputs(seed))
    spreads = {'L0_attn_bq': (0.0, 0.8),
     'L0_attn_bk': (0.0, 0.8),
     'L0_attn_bv': (0.0, 0.1),
     'L0_attn_bo': (0.0, 0.1)}
    factors = {'L0_attn_wq': 3.95, 'L0_ffn_W_r': 3.196, 'L0_ffn_mu_r': 6.319}
    for name, (base, spread) in spreads.items():
        noise = np.random.default_rng([zlib.crc32(name.encode()), seed]).standard_normal(out[name].shape)
        drawn = base * np.exp(spread * noise) if base else spread * noise
        out[name] = jnp.asarray(drawn.astype(out[name].dtype))
    for name, factor in factors.items():
        out[name] = (out[name] * factor).astype(out[name].dtype)
    return out
```

```python
import numpy as np
import concourse.bass as bass
from concourse import mybir
from contextlib import ExitStack

W_R, W_K, W_V, WQ, WK, WV, WO = range(7)
MU_R, MU_K, BQ = range(3)
BK, BV, BO = range(3)
HEADS = 16
LN_EPS = 1e-5
DEN_EPS = 1e-6


def macaron_block(nc: bass.Bass, x: bass.AP, weights: bass.AP, columns: bass.AP, rows: bass.AP, out: bass.AP):
    fp32 = mybir.dt.float32
    bf16 = mybir.dt.bfloat16
    ALU = mybir.AluOpType
    ACT = mybir.ActivationFunctionType

    B, S, D = x.shape
    P = 128
    T = S // P
    DH = D // HEADS
    assert D == P and S == 512
    UNITS = 3 * B
    MV = nc.vector.BN_AGGR_DIM

    def ffn(u):
        return 0 <= u < B or 2 * B <= u < UNITS

    def att(u):
        return B <= u < 2 * B

    def layers(u):
        return u + 1 if u < B else B if u < 2 * B else u + 1 - B

    def atts(u):
        return min(max(u + 1 - B, 0), B)

    ctx = ExitStack()
    with ctx:
        def sb(name, shape, dt=fp32):
            return ctx.enter_context(nc.sbuf_tensor(name, shape, dt))

        def sem(name):
            return ctx.enter_context(nc.semaphore(name))

        X = sb("X", [P, B, T, D])
        W = sb("W", [P, 7, D])
        Wv4 = sb("Wv4", [P, D])
        COL = sb("COL", [P, 3])
        ROW = sb("ROW", [P, 3, D])
        ident = sb("ident", [P, P])
        head_mask = sb("head_mask", [P, HEADS, DH])
        head_of = sb("head_of", [P, HEADS])
        ones = sb("ones", [P, 1])
        minus_half = sb("minus_half", [P, T])
        third = sb("third", [P, P], bf16)
        bias_k = sb("bias_k", [P, T, D], bf16)
        bias_o = sb("bias_o", [P, T, D], bf16)
        part = [[sb(f"part{i}{n}", [P, D], bf16 if n < 2 else fp32) for n in range(4)] for i in range(2)]

        def ring(name, n, shape):
            return [sb(f"{name}{i}", shape) for i in range(n)]

        stats = ring("stats", 4, [P, T, nc.vector.BN_STATS_DIM])
        mean_var = ring("mean_var", 4, [P, T, MV])
        var_eps = ring("var_eps", 4, [P, T])
        rstd = ring("rstd", 4, [P, T])
        xn = ring("xn", 4, [P, T, D])
        xnT = ring("xnT", 3, [P, 1 + S])
        diff = ring("diff", 2, [P, S])
        xkT = ring("xkT", 2, [P, S])
        xrT = ring("xrT", 2, [P, S])
        kpos = ring("kpos", 2, [P, S])
        kact = ring("kact", 2, [P, S])
        gate = ring("gate", 2, [P, T, D])
        gated = ring("gated", 2, [P, T, D])
        ek = ring("ek", 2, [P, T, D])
        rk = ring("rk", 2, [P, T, D])
        kf = ring("kf", 2, [P, T, D])
        eq = ring("eq", 2, [P, S])
        rq = ring("rq", 2, [P, S])
        qfT = ring("qfT", 2, [P, S])
        gram = ring("gram", 2, [P, D])
        ksum_diag = ring("ksum_diag", 2, [P, D])
        ksum_head = ring("ksum_head", 2, [P, HEADS])
        kvT = ring("kvT", 2, [P, D])
        kvo = ring("kvo", 2, [P, D])
        den = ring("den", 2, [P, T, HEADS])
        z = ring("z", 2, [P, T, HEADS])
        z_wide = ring("z_wide", 2, [P, T, HEADS, DH])
        qzT = ring("qzT", 2, [P, S])

        bank = [ctx.enter_context(nc.psum_tensor(f"bank{i}", [P, 512], fp32)) for i in range(8)]
        bank_T = bank[0:2]
        bank_K, bank_R, bank_V = bank[2:4], bank[4:6], bank[6:8]
        bank_k, bank_q, bank_d, bank_z, bank_g, bank_o = bank[2:8]

        x_loaded = [sem(f"x_loaded{c}") for c in range(B)]
        consts_loaded = sem("consts_loaded")
        id_made = sem("id_made")
        masks_made = sem("masks_made")
        pool_step = sem("pool_step")
        bias_ready = sem("bias_ready")
        bias_step = sem("bias_step")
        setup_done = sem("setup_done")
        stats_done = sem("stats_done")
        mean_var_ready = sem("mean_var_ready")
        var_eps_done = sem("var_eps_done")
        rstd_ready = sem("rstd_ready")
        xn_ready = sem("xn_ready")
        t_ready = sem("t_ready")
        xnT_ready = sem("xnT_ready")
        diff_ready = sem("diff_ready")
        xk_ready = sem("xk_ready")
        xr_ready = sem("xr_ready")
        k_ready = sem("k_ready")
        r_ready = sem("r_ready")
        kpos_done = sem("kpos_done")
        kact_ready = sem("kact_ready")
        gate_ready = sem("gate_ready")
        v_ready = sem("v_ready")
        gated_ready = sem("gated_ready")
        x_gated = sem("x_gated")
        ak_ready = sem("ak_ready")
        aq_ready = sem("aq_ready")
        ek_ready = sem("ek_ready")
        eq_ready = sem("eq_ready")
        kf_ready = sem("kf_ready")
        qf_ready = sem("qf_ready")
        gram_ps_ready = sem("gram_ps_ready")
        ksum_ps_ready = sem("ksum_ps_ready")
        gram_ready = sem("gram_ready")
        ksum_ready = sem("ksum_ready")
        kvT_ps_ready = sem("kvT_ps_ready")
        kvT_ready = sem("kvT_ready")
        den_ps_ready = sem("den_ps_ready")
        den_done = sem("den_done")
        z_ready = sem("z_ready")
        z_wide_ready = sem("z_wide_ready")
        zT_ready = sem("zT_ready")
        kvo_ps_ready = sem("kvo_ps_ready")
        kvo_ready = sem("kvo_ready")
        qz_ready = sem("qz_ready")
        o_ready = sem("o_ready")
        x_attended = sem("x_attended")
        stored = sem("stored")

        N_CONST = 3
        STEPS = range(-4, UNITS + 1)

        block = ctx.enter_context(nc.Block())

        def tiles(ap):
            return ap.rearrange("(t p) d -> p t d", p=P)

        @block.sync
        def _(sp):
            for c in range(B):
                sp.dma_start(X[:, c], tiles(x[c])).then_inc(x_loaded[c], 16)
            for c in range(B):
                sp.wait_ge(x_gated, B + c + 1)
                sp.dma_start(tiles(out[c]), X[:, c]).then_inc(stored, 16)
            sp.wait_ge(stored, 16 * B)

        @block.gpsimd
        def _(pool):
            nc.gpsimd.memset(ident[:], 0.0).then_inc(pool_step, 1)
            nc.gpsimd.memset(minus_half[:], -0.5).then_inc(pool_step, 1)
            pool.wait_ge(pool_step, 2)
            nc.gpsimd.affine_select(out=ident[:], in_=ident[:], compare_op=ALU.not_equal, fill=1.0, base=0,
                                    pattern=[[-1, P]], channel_multiplier=1).then_inc(id_made, 1)

            def rstd_of(u):
                r = u % 4
                pool.wait_ge(mean_var_ready, u + 1)
                nc.gpsimd.tensor_scalar(var_eps[r][:], mean_var[r][:, :, 1], 1.0, LN_EPS, ALU.mult,
                                        ALU.add).then_inc(var_eps_done, 1)
                pool.wait_ge(var_eps_done, u + 1)
                nc.gpsimd.tensor_tensor(rstd[r][:], var_eps[r][:], minus_half[:], ALU.pow).then_inc(rstd_ready, 1)

            def difference(u):
                n = layers(u)
                pool.wait_ge(xnT_ready, u + 1)
                if n > 2:
                    pool.wait_ge(xr_ready, n - 2)
                nc.gpsimd.tensor_tensor(diff[u % 2][:], xnT[u % 3][:, 1:1 + S], xnT[u % 3][:, 0:S],
                                        ALU.subtract).then_inc(diff_ready, 1)

            def add_gated(u):
                pool.wait_ge(gated_ready, layers(u))
                nc.gpsimd.tensor_tensor(X[:, u % B], X[:, u % B], gated[u % 2][:], ALU.add).then_inc(x_gated, 1)

            def masks():
                nc.gpsimd.memset(head_mask[:], 1.0).then_inc(pool_step, 1)
                nc.gpsimd.memset(head_of[:], 1.0).then_inc(pool_step, 1)
                pool.wait_ge(pool_step, 4)
                for lo in range(2):
                    base, sign = ((0, 1), (DH - 1, -1))[lo]
                    nc.gpsimd.affine_select(out=head_mask[:], in_=head_mask[:], compare_op=ALU.is_ge, fill=0.0,
                                            base=base, pattern=[[-sign * DH, HEADS], [0, DH]],
                                            channel_multiplier=sign).then_inc(masks_made, 1)
                    nc.gpsimd.affine_select(out=head_of[:], in_=head_of[:], compare_op=ALU.is_ge, fill=0.0,
                                            base=base, pattern=[[-sign * DH, HEADS]],
                                            channel_multiplier=sign).then_inc(masks_made, 1)
                    pool.wait_ge(masks_made, 2 * lo + 2)

            for s in STEPS:
                if 0 <= s + 4 < UNITS:
                    rstd_of(s + 4)
                if s == 0:
                    masks()
                if ffn(s + 2):
                    difference(s + 2)
                if ffn(s):
                    add_gated(s)

        @block.scalar
        def _(act):
            act.dma_start(COL[:], columns).then_inc(consts_loaded, 16)
            act.dma_start(W[:], weights.rearrange("(i p) d -> p i d", p=P)).then_inc(consts_loaded, 16)
            act.dma_start(ROW[:], rows.partition_broadcast(P)).then_inc(consts_loaded, 16)

            def take_xnT(u):
                act.wait_ge(t_ready, u + 1)
                if u == 0:
                    act.wait_ge(setup_done, 1)
                if u >= 3:
                    v = u - 3
                    if ffn(v):
                        act.wait_ge(xr_ready, layers(v))
                    else:
                        act.wait_ge(aq_ready, atts(v))
                nc.scalar.activation(xnT[u % 3][:, 1:1 + S], bank_T[u % 2][:], ACT.Copy).then_inc(xnT_ready, 1)

            def relu_k(u):
                n = layers(u)
                act.wait_ge(k_ready, n)
                if n > 2:
                    act.wait_ge(kact_ready, n - 2)
                nc.scalar.activation(kpos[u % 2][:], bank_K[u % 2][:], ACT.Relu).then_inc(kpos_done, 1)

            def square_k(u):
                n = layers(u)
                act.wait_ge(kpos_done, n)
                if n > 2:
                    act.wait_ge(v_ready, n - 2)
                nc.scalar.activation(kact[u % 2][:], kpos[u % 2][:], ACT.Square).then_inc(kact_ready, 1)

            def gate_of(u):
                n = layers(u)
                act.wait_ge(r_ready, n)
                if n > 2:
                    act.wait_ge(gated_ready, n - 2)
                nc.scalar.activation(gate[u % 2][:].rearrange("p t d -> p (t d)"), bank_R[u % 2][:], ACT.Tanh,
                                     scale=0.5).then_inc(gate_ready, 1)

            def features_k(u):
                n = atts(u)
                act.wait_ge(ak_ready, n)
                if n > 2:
                    act.wait_ge(kf_ready, n - 2)
                flat = [r[u % 2][:].rearrange("p t d -> p (t d)") for r in (ek, rk)]
                nc.scalar.activation(flat[0], bank_k[:], ACT.Exp)
                nc.scalar.activation(flat[1], bank_k[:], ACT.Relu).then_inc(ek_ready, 1)

            def features_q(u):
                n = atts(u)
                act.wait_ge(aq_ready, n)
                if n > 2:
                    act.wait_ge(qf_ready, n - 2)
                nc.scalar.activation(eq[u % 2][:], bank_q[:], ACT.Exp, bias=COL[:, BQ:BQ + 1])
                nc.scalar.activation(rq[u % 2][:], bank_q[:], ACT.Relu, bias=COL[:, BQ:BQ + 1]).then_inc(eq_ready, 1)

            def widen_z(u):
                n = atts(u)
                act.wait_ge(z_ready, n)
                if n > 2:
                    act.wait_ge(zT_ready, n - 2)
                nc.scalar.activation(z_wide[u % 2][:].rearrange("p t h e -> p (t h) e"),
                                     z[u % 2][:].rearrange("p t h -> p (t h)").unsqueeze(2).to_broadcast([P, T * HEADS, DH]),
                                     ACT.Copy).then_inc(z_wide_ready, 1)

            def take_gram(u):
                n = atts(u)
                act.wait_ge(gram_ps_ready, n)
                nc.scalar.activation(gram[u % 2][:], bank_g[:, 0:D], ACT.Copy).then_inc(gram_ready, 1)

            def take_kvo(u):
                n = atts(u)
                act.wait_ge(kvo_ps_ready, n)
                if n > 2:
                    act.wait_ge(o_ready, n - 2)
                nc.scalar.activation(kvo[u % 2][:], bank_g[:, 0:D], ACT.Copy).then_inc(kvo_ready, 1)

            for s in STEPS:
                if ffn(s):
                    if s == 0:
                        act.wait_ge(consts_loaded, 16 * N_CONST)
                    relu_k(s)
                    square_k(s)
                    gate_of(s)
                if att(s):
                    features_k(s)
                if att(s - 1):
                    widen_z(s - 1)
                if att(s):
                    features_q(s)
                if att(s - 1):
                    take_kvo(s - 1)
                if 0 <= s + 2 < UNITS:
                    take_xnT(s + 2)
                if att(s):
                    take_gram(s)

        @block.vector
        def _(dve):
            for r in range(3):
                nc.vector.memset(xnT[r][:, 0:1], 0.0)
            nc.vector.memset(ones[:], 1.0)
            nc.vector.memset(third[:], 1.0 / 32).then_inc(setup_done, 1)

            def stats_of(u):
                r, c = u % 4, u % B
                if u < B:
                    dve.wait_ge(x_loaded[c], 16)
                elif u < 2 * B:
                    dve.wait_ge(x_gated, c + 1)
                else:
                    dve.wait_ge(x_attended, c + 1)
                if u >= 4:
                    dve.wait_ge(rstd_ready, u - 3)
                for t in range(T):
                    last = nc.vector.bn_stats(stats[r][:, t, :], X[:, c, t, :])
                last.then_inc(stats_done, 1)
                dve.wait_ge(stats_done, u + 1)
                for t in range(T):
                    last = nc.vector.bn_aggr(mean_var[r][:, t, :], stats[r][:, t, :])
                last.then_inc(mean_var_ready, 1)

            def normalize(u):
                r, c = u % 4, u % B
                dve.wait_ge(rstd_ready, u + 1)
                if u >= 4:
                    dve.wait_ge(t_ready, u - 3)
                    if att(u - 4):
                        dve.wait_ge(gram_ps_ready, atts(u - 4))
                for t in range(T):
                    last = nc.vector.tensor_scalar(xn[r][:, t, :], X[:, c, t, :], mean_var[r][:, t, 0:1],
                                                   rstd[r][:, t:t + 1], ALU.subtract, ALU.mult)
                last.then_inc(xn_ready, 1)

            def mix(u):
                n = layers(u)
                prev = xnT[u % 3][:, 0:S]
                dve.wait_ge(diff_ready, n)
                if n > 2:
                    dve.wait_ge(k_ready, n - 2)
                nc.vector.scalar_tensor_tensor(out=xkT[u % 2][:], in0=diff[u % 2][:], scalar=COL[:, MU_K:MU_K + 1],
                                               in1=prev, op0=ALU.mult, op1=ALU.add).then_inc(xk_ready, 1)
                if n > 2:
                    dve.wait_ge(r_ready, n - 2)
                nc.vector.scalar_tensor_tensor(out=xrT[u % 2][:], in0=diff[u % 2][:], scalar=COL[:, MU_R:MU_R + 1],
                                               in1=prev, op0=ALU.mult, op1=ALU.add).then_inc(xr_ready, 1)

            def gate_values(u):
                n = layers(u)
                dve.wait_ge(v_ready, n)
                dve.wait_ge(gate_ready, n)
                if n > 2:
                    dve.wait_ge(x_gated, n - 2)
                nc.vector.scalar_tensor_tensor(out=gated[u % 2][:].rearrange("p t d -> p (t d)"),
                                               in0=gate[u % 2][:].rearrange("p t d -> p (t d)"), scalar=1.0,
                                               in1=bank_V[u % 2][:], op0=ALU.add, op1=ALU.mult).then_inc(gated_ready, 1)

            def features_k(u):
                n = atts(u)
                dve.wait_ge(ek_ready, n)
                if n > 2:
                    dve.wait_ge(ksum_ps_ready, n - 2)
                nc.vector.scalar_tensor_tensor(out=kf[u % 2][:], in0=ek[u % 2][:], scalar=1.0, in1=rk[u % 2][:],
                                               op0=ALU.min, op1=ALU.add).then_inc(kf_ready, 1)

            def features_q(u):
                n = atts(u)
                dve.wait_ge(eq_ready, n)
                nc.vector.scalar_tensor_tensor(out=qfT[u % 2][:], in0=eq[u % 2][:], scalar=1.0, in1=rq[u % 2][:],
                                               op0=ALU.min, op1=ALU.add).then_inc(qf_ready, 1)

            def spread_ksum(u):
                n = atts(u)
                dve.wait_ge(ksum_ps_ready, n)
                if n == 1:
                    dve.wait_ge(masks_made, 4)
                nc.vector.tensor_scalar(ksum_diag[u % 2][:], ident[:], bank_d[:, 0:1], None, ALU.mult)
                nc.vector.tensor_scalar(ksum_head[u % 2][:], head_of[:], bank_d[:, 0:1], None,
                                        ALU.mult).then_inc(ksum_ready, 1)

            def mask_kv(u):
                n = atts(u)
                dve.wait_ge(kvT_ps_ready, n)
                nc.vector.tensor_tensor(kvT[u % 2][:], bank_g[:, 0:D], head_mask[:].rearrange("p h e -> p (h e)"),
                                        ALU.mult).then_inc(kvT_ready, 1)

            def z_of(u):
                n = atts(u)
                dve.wait_ge(den_ps_ready, n)
                nc.vector.tensor_scalar(den[u % 2][:].rearrange("p t h -> p (t h)"), bank_d[:, 64:64 + T * HEADS],
                                        DEN_EPS, None, ALU.add).then_inc(den_done, 1)
                dve.wait_ge(den_done, n)
                nc.vector.reciprocal(z[u % 2][:], den[u % 2][:]).then_inc(z_ready, 1)

            def scale_q(u):
                n = atts(u)
                dve.wait_ge(zT_ready, n)
                nc.vector.tensor_tensor(qzT[u % 2][:], qfT[u % 2][:], bank_z[:], ALU.mult).then_inc(qz_ready, 1)

            def add_attended(u):
                n = atts(u)
                dve.wait_ge(o_ready, n)
                xc = X[:, u % B].rearrange("p t d -> p (t d)")
                nc.vector.tensor_tensor(xc, xc, bank_o[:], ALU.add).then_inc(x_attended, 1)

            def split_bias(i, row, bias):
                a, b, rest, rest2 = part[i]
                k = 3 * i
                R = ROW[:, row, :]
                nc.vector.tensor_copy(a[:], R).then_inc(bias_step, 1)
                dve.wait_ge(bias_step, k + 1)
                nc.vector.tensor_tensor(rest[:], R, a[:], ALU.subtract).then_inc(bias_step, 1)
                dve.wait_ge(bias_step, k + 2)
                nc.vector.tensor_copy(b[:], rest[:]).then_inc(bias_step, 1)
                dve.wait_ge(bias_step, k + 3)
                nc.vector.tensor_tensor(rest2[:], rest[:], b[:], ALU.subtract).then_inc(bias_ready, 1)
                dve.wait_ge(bias_ready, 2 * i + 1)
                for q, p in enumerate((a, b, rest2)):
                    rows32 = slice(32 * q, 32 * q + 32)
                    nc.vector.tensor_copy(bias[rows32], p[rows32].unsqueeze(1).to_broadcast([32, T, D]))
                nc.vector.memset(bias[96:128], 0.0).then_inc(bias_ready, 1)

            for s in STEPS:
                if att(s - 1):
                    mask_kv(s - 1)
                    z_of(s - 1)
                if s == -2:
                    dve.wait_ge(consts_loaded, 16 * N_CONST)
                    nc.vector.tensor_scalar(Wv4[:], W[:, W_V, :], 0.25, None, ALU.mult).then_inc(setup_done, 1)
                if s == 1:
                    split_bias(0, BK, bias_k)
                    split_bias(1, BO, bias_o)
                if ffn(s + 1):
                    mix(s + 1)
                if att(s):
                    features_k(s)
                if 0 <= s + 4 < UNITS:
                    stats_of(s + 4)
                if att(s - 1):
                    scale_q(s - 1)
                if att(s):
                    features_q(s)
                if 0 <= s + 3 < UNITS:
                    normalize(s + 3)
                if ffn(s):
                    gate_values(s)
                if att(s):
                    spread_ksum(s)
                if att(s - 1):
                    add_attended(s - 1)

        @block.tensor
        def _(pe):
            def transpose_x(u):
                pe.wait_ge(xn_ready, u + 1)
                if u >= 2:
                    pe.wait_ge(xnT_ready, u - 1)
                for t in range(T):
                    last = nc.tensor.transpose(bank_T[u % 2][:, t * P:(t + 1) * P], xn[u % 4][:, t, :], ident[:])
                last.then_inc(t_ready, 1)

            def ffn_k(u):
                n = layers(u)
                pe.wait_ge(xk_ready, n)
                if n > 2:
                    pe.wait_ge(kpos_done, n - 2)
                if u == 2 * B:
                    pe.wait_ge(ek_ready, B)
                if u == 2 * B + 1:
                    pe.wait_ge(eq_ready, B)
                nc.tensor.matmul(bank_K[u % 2][:], W[:, W_K, :], xkT[u % 2][:], start=True, stop=True).then_inc(k_ready, 1)

            def ffn_r(u):
                n = layers(u)
                pe.wait_ge(xr_ready, n)
                if n > 2:
                    pe.wait_ge(gate_ready, n - 2)
                if u == 2 * B:
                    pe.wait_ge(den_done, B)
                if u == 2 * B + 1:
                    pe.wait_ge(qz_ready, B)
                for t in range(T):
                    last = nc.tensor.matmul(bank_R[u % 2][:, t * P:(t + 1) * P], xrT[u % 2][:, t * P:(t + 1) * P],
                                            W[:, W_R, :], start=True, stop=True)
                last.then_inc(r_ready, 1)

            def ffn_v(u):
                n = layers(u)
                pe.wait_ge(kact_ready, n)
                if n > 2:
                    pe.wait_ge(gated_ready, n - 2)
                if u == 2 * B:
                    pe.wait_ge(kvo_ready, B)
                if u == 2 * B + 1:
                    pe.wait_ge(x_attended, B)
                for t in range(T):
                    last = nc.tensor.matmul(bank_V[u % 2][:, t * P:(t + 1) * P], kact[u % 2][:, t * P:(t + 1) * P],
                                            Wv4[:], start=True, stop=True)
                last.then_inc(v_ready, 1)

            def att_k(u):
                n = atts(u)
                pe.wait_ge(xnT_ready, u + 1)
                if n == 1:
                    pe.wait_ge(bias_ready, 4)
                    pe.wait_ge(kpos_done, B)
                if n > 1:
                    pe.wait_ge(ek_ready, n - 1)
                nc.tensor.matmul(bank_k[:], third[:], bias_k[:].rearrange("p t d -> p (t d)"), start=True, stop=False)
                for t in range(T):
                    last = nc.tensor.matmul(bank_k[:, t * P:(t + 1) * P], xnT[u % 3][:, 1 + t * P:1 + (t + 1) * P],
                                            W[:, WK, :], start=False, stop=(t == T - 1))
                last.then_inc(ak_ready, 1)

            def att_q(u):
                n = atts(u)
                if n > 1:
                    pe.wait_ge(eq_ready, n - 1)
                nc.tensor.matmul(bank_q[:], W[:, WQ, :], xnT[u % 3][:, 1:1 + S], start=True, stop=True).then_inc(aq_ready, 1)

            def att_gram(u):
                n = atts(u)
                pe.wait_ge(kf_ready, n)
                if n == 1:
                    pe.wait_ge(gated_ready, B)
                    pe.wait_ge(gate_ready, B)
                if n > 1:
                    pe.wait_ge(kvo_ready, n - 1)
                for t in range(T):
                    last = nc.tensor.matmul(bank_g[:, 0:D], xn[u % 4][:, t, :], kf[u % 2][:, t, :],
                                            start=(t == 0), stop=(t == T - 1))
                last.then_inc(gram_ps_ready, 1)
                if n > 1:
                    pe.wait_ge(den_done, n - 1)
                for t in range(T):
                    last = nc.tensor.matmul(bank_d[:, 0:1], kf[u % 2][:, t, :], ones[:], start=(t == 0), stop=(t == T - 1))
                last.then_inc(ksum_ps_ready, 1)

            def att_kv(u):
                n = atts(u)
                pe.wait_ge(gram_ready, n)
                pe.wait_ge(ksum_ready, n)
                nc.tensor.matmul(bank_g[:, 0:D], W[:, WV, :], gram[u % 2][:], start=True, stop=False)
                nc.tensor.matmul(bank_g[:, 0:D], ROW[:, BV, :], ksum_diag[u % 2][:], start=False,
                                 stop=True).then_inc(kvT_ps_ready, 1)

            def att_den(u):
                n = atts(u)
                pe.wait_ge(qf_ready, n)
                for t in range(T):
                    last = nc.tensor.matmul(bank_d[:, 64 + t * HEADS:64 + (t + 1) * HEADS],
                                            qfT[u % 2][:, t * P:(t + 1) * P], ksum_head[u % 2][:], start=True, stop=True)
                last.then_inc(den_ps_ready, 1)

            def att_z(u):
                n = atts(u)
                pe.wait_ge(z_wide_ready, n)
                if n > 1:
                    pe.wait_ge(qz_ready, n - 1)
                for t in range(T):
                    last = nc.tensor.transpose(bank_z[:, t * P:(t + 1) * P],
                                               z_wide[u % 2][:, t].rearrange("p h e -> p (h e)"), ident[:])
                last.then_inc(zT_ready, 1)

            def att_kvo(u):
                n = atts(u)
                pe.wait_ge(kvT_ready, n)
                nc.tensor.matmul(bank_g[:, 0:D], kvT[u % 2][:], W[:, WO, :], start=True, stop=True).then_inc(kvo_ps_ready, 1)

            def att_out(u):
                n = atts(u)
                pe.wait_ge(kvo_ready, n)
                pe.wait_ge(qz_ready, n)
                if n > 1:
                    pe.wait_ge(x_attended, n - 1)
                nc.tensor.matmul(bank_o[:], third[:], bias_o[:].rearrange("p t d -> p (t d)"), start=True, stop=False)
                for t in range(T):
                    last = nc.tensor.matmul(bank_o[:, t * P:(t + 1) * P], qzT[u % 2][:, t * P:(t + 1) * P],
                                            kvo[u % 2][:], start=False, stop=(t == T - 1))
                last.then_inc(o_ready, 1)

            pe.wait_ge(id_made, 1)
            for s in STEPS:
                if s == 0:
                    pe.wait_ge(setup_done, 2)
                if att(s - 1):
                    att_kv(s - 1)
                    att_den(s - 1)
                if ffn(s):
                    ffn_k(s)
                    ffn_r(s)
                if att(s):
                    att_k(s)
                    att_q(s)
                if att(s - 1):
                    att_z(s - 1)
                    att_kvo(s - 1)
                if 0 <= s + 2 < UNITS:
                    transpose_x(s + 2)
                if ffn(s):
                    ffn_v(s)
                if att(s):
                    att_gram(s)
                if att(s - 1):
                    att_out(s - 1)


def kernel(**inputs):
    import concourse.bacc as bacc
    from concourse.bass_utils import run_bass_kernel_spmd as run

    given = {k: np.ascontiguousarray(v) for k, v in inputs.items()}
    arrays = {
        "x": given["L0_attn_x"],
        "weights": np.concatenate([given[f"L0_ffn_{n}"].T for n in ("W_r", "W_k", "W_v")]
                                  + [given[f"L0_attn_{n}"] for n in ("wq", "wk", "wv", "wo")], axis=0),
        "columns": np.stack([given["L0_ffn_mu_r"], given["L0_ffn_mu_k"], given["L0_attn_bq"]], axis=1),
        "rows": np.stack([given["L0_attn_bk"], given["L0_attn_bv"], given["L0_attn_bo"]], axis=0),
    }
    arrays = {k: np.ascontiguousarray(v) for k, v in arrays.items()}
    nc = bacc.Bacc("TRN2", target_bir_lowering=False, num_devices=1)
    args = [nc.dram_tensor(k, v.shape, mybir.dt.from_np(v.dtype), kind="ExternalInput").ap() for k, v in arrays.items()]
    out = nc.dram_tensor("out", arrays["x"].shape, mybir.dt.float32, kind="ExternalOutput").ap()
    macaron_block(nc, *args, out)
    r = run(nc, [arrays], core_ids=[0])
    return r.results[0]["out"]
```

```python
import numpy as np
import concourse.bass as bass
from concourse import mybir
from contextlib import ExitStack

W_R, W_K, W_V, WQ, WK, WV, WO = range(7)
MU_R, MU_K, BQ, BV = range(4)
BK, BO = range(2)
HEADS = 16
LN_EPS = 1e-5
DEN_EPS = 1e-6


def macaron_block(nc: bass.Bass, x: bass.AP, weights: bass.AP, columns: bass.AP, rows: bass.AP, out: bass.AP):
    fp32 = mybir.dt.float32
    bf16 = mybir.dt.bfloat16
    ALU = mybir.AluOpType
    ACT = mybir.ActivationFunctionType

    B, S, D = x.shape
    P = 128
    T = S // P
    DH = D // HEADS
    assert D == P and S == 512
    UNITS = 3 * B
    MV = nc.vector.BN_AGGR_DIM

    def ffn(u):
        return 0 <= u < B or 2 * B <= u < UNITS

    def att(u):
        return B <= u < 2 * B

    def layers(u):
        return u + 1 if u < B else B if u < 2 * B else u + 1 - B

    def atts(u):
        return min(max(u + 1 - B, 0), B)

    def act_tiles(u):
        return range(1, T) if att(u) else range(2, T)

    ctx = ExitStack()
    with ctx:
        def sb(name, shape, dt=fp32):
            return ctx.enter_context(nc.sbuf_tensor(name, shape, dt))

        def sem(name):
            return ctx.enter_context(nc.semaphore(name))

        X = sb("X", [P, B, T, D])
        W = sb("W", [P, 7, D])
        Wv4 = sb("Wv4", [P, D])
        COL = sb("COL", [P, 4])
        ROW = sb("ROW", [P, 2, D])
        prev_mu = sb("prev_mu", [P, 2])
        bv_heads = sb("bv_heads", [P, D])
        bv_wo = sb("bv_wo", [P, D])
        ident = sb("ident", [P, P])
        head_mask = sb("head_mask", [P, HEADS, DH])
        head_of = sb("head_of", [P, HEADS])
        ones = sb("ones", [P, 1])
        minus_half = sb("minus_half", [P, T])
        third = sb("third", [P, P], bf16)
        bias_k = sb("bias_k", [P, T, D], bf16)
        part = [sb(f"part{n}", [P, D], bf16 if n < 2 else fp32) for n in range(4)]

        def ring(name, n, shape):
            return [sb(f"{name}{i}", shape) for i in range(n)]

        stats = ring("stats", 4, [P, T, nc.vector.BN_STATS_DIM])
        mean_var = ring("mean_var", 4, [P, T, MV])
        var_eps = ring("var_eps", 4, [P, T])
        rstd = ring("rstd", 4, [P, T])
        neg_mean = ring("neg_mean", 4, [P, T])
        shift = ring("shift", 4, [P, T])
        xn = ring("xn", 4, [P, T, D])
        xnT = ring("xnT", 3, [P, S])
        xkT = ring("xkT", 2, [P, S])
        xrT = ring("xrT", 2, [P, S])
        kpos = ring("kpos", 2, [P, S])
        kact = ring("kact", 2, [P, S])
        gate = ring("gate", 2, [P, T, D])
        gated = ring("gated", 2, [P, T, D])
        ek = ring("ek", 2, [P, T, D])
        rk = ring("rk", 2, [P, T, D])
        kf = ring("kf", 2, [P, T, D])
        eq = ring("eq", 2, [P, S])
        rq = ring("rq", 2, [P, S])
        qfT = ring("qfT", 2, [P, S])
        gram = ring("gram", 2, [P, D])
        kf2 = ring("kf2", 2, [P, T // 2, D])
        kf1 = ring("kf1", 2, [P, D])
        ksum = ring("ksum", 2, [P, 1])
        ksum_head = ring("ksum_head", 2, [P, HEADS])
        kvT = ring("kvT", 2, [P, D])
        kvo = ring("kvo", 2, [P, D])
        den = ring("den", 2, [P, T, HEADS])
        z = ring("z", 2, [P, T, HEADS])
        z_wide = ring("z_wide", 2, [P, T, HEADS, DH])
        qzT = ring("qzT", 2, [P, S])

        bank = [ctx.enter_context(nc.psum_tensor(f"bank{i}", [P, 512], fp32)) for i in range(8)]
        bank_T = bank[0:2]
        bank_K, bank_R, bank_V = bank[2:4], bank[4:6], bank[6:8]
        bank_k, bank_q, bank_d = bank[2], bank[4], bank[6]
        bank_g, bank_z, bank_o = bank[3], bank[5], bank[7]

        x_loaded = [sem(f"x_loaded{c}") for c in range(B)]
        columns_loaded = sem("columns_loaded")
        weights_loaded = sem("weights_loaded")
        rows_loaded = sem("rows_loaded")
        x_gated_last = sem("x_gated_last")
        id_made = sem("id_made")
        masks_made = sem("masks_made")
        pool_step = sem("pool_step")
        bias_ready = sem("bias_ready")
        bias_step = sem("bias_step")
        setup_done = sem("setup_done")
        stats_done = sem("stats_done")
        mean_var_ready = sem("mean_var_ready")
        var_eps_done = sem("var_eps_done")
        rstd_ready = sem("rstd_ready")
        xn_ready = sem("xn_ready")
        t_ready = sem("t_ready")
        xnT_ready = sem("xnT_ready")
        mu_x_ready = sem("mu_x_ready")
        shift_ready = sem("shift_ready")
        xn_act_ready = sem("xn_act_ready")
        bo_added = sem("bo_added")
        kf2_done = sem("kf2_done")
        kf1_ready = sem("kf1_ready")
        bv_wo_ps_ready = sem("bv_wo_ps_ready")
        bv_wo_ready = sem("bv_wo_ready")
        xk_ready = sem("xk_ready")
        xr_ready = sem("xr_ready")
        k_ready = sem("k_ready")
        r_ready = sem("r_ready")
        kpos_done = sem("kpos_done")
        kact_ready = sem("kact_ready")
        gate_ready = sem("gate_ready")
        v_ready = sem("v_ready")
        gated_ready = sem("gated_ready")
        x_gated = sem("x_gated")
        ak_ready = sem("ak_ready")
        aq_ready = sem("aq_ready")
        ek_ready = sem("ek_ready")
        eq_ready = sem("eq_ready")
        kf_ready = sem("kf_ready")
        qf_ready = sem("qf_ready")
        gram_ps_ready = sem("gram_ps_ready")
        ksum_ps_ready = sem("ksum_ps_ready")
        gram_ready = sem("gram_ready")
        ksum_ready = sem("ksum_ready")
        kvT_ps_ready = sem("kvT_ps_ready")
        kvT_ready = sem("kvT_ready")
        den_ps_ready = sem("den_ps_ready")
        den_done = sem("den_done")
        z_ready = sem("z_ready")
        z_wide_ready = sem("z_wide_ready")
        zT_ready = sem("zT_ready")
        kvo_ps_ready = sem("kvo_ps_ready")
        kvo_ready = sem("kvo_ready")
        qz_ready = sem("qz_ready")
        o_ready = sem("o_ready")
        x_attended = sem("x_attended")
        stored = sem("stored")

        WARM = {0: 50, -2: 10, -1: 15}
        BY_VECTOR = (UNITS - 1,)
        STEPS = range(-5, UNITS + 2)

        block = ctx.enter_context(nc.Block())

        def tiles(ap):
            return ap.rearrange("(t p) d -> p t d", p=P)

        @block.sync
        def _(sp):
            for c in range(B):
                sp.dma_start(X[:, c], tiles(x[c])).then_inc(x_loaded[c], 16)
            for c in range(B):
                if 2 * B + c in BY_VECTOR:
                    sp.wait_ge(x_gated_last, 1)
                else:
                    sp.wait_ge(x_gated, B + c + 1)
                sp.dma_start(tiles(out[c]), X[:, c]).then_inc(stored, 16)
            sp.wait_ge(stored, 16 * B)

        @block.gpsimd
        def _(pool):
            nc.gpsimd.memset(ident[:], 0.0).then_inc(pool_step, 1)
            nc.gpsimd.memset(minus_half[:], -0.5).then_inc(pool_step, 1)
            pool.wait_ge(pool_step, 2)
            nc.gpsimd.affine_select(out=ident[:], in_=ident[:], compare_op=ALU.not_equal, fill=1.0, base=0,
                                    pattern=[[-1, P]], channel_multiplier=1).then_inc(id_made, 1)

            def rstd_of(u):
                r = u % 4
                pool.wait_ge(mean_var_ready, u + 1)
                if u >= 4:
                    pool.wait_ge(xn_act_ready, u - 3)
                nc.gpsimd.tensor_scalar(var_eps[r][:], mean_var[r][:, :, 1], 1.0, LN_EPS, ALU.mult,
                                        ALU.add).then_inc(var_eps_done, 1)
                nc.gpsimd.tensor_scalar(neg_mean[r][:], mean_var[r][:, :, 0], -1.0, 0.0, ALU.mult, ALU.add)
                pool.wait_ge(var_eps_done, u + 1)
                nc.gpsimd.tensor_tensor(rstd[r][:], var_eps[r][:], minus_half[:], ALU.pow).then_inc(rstd_ready, 1)
                pool.wait_ge(rstd_ready, u + 1)
                nc.gpsimd.tensor_tensor(shift[r][:], neg_mean[r][:], rstd[r][:], ALU.mult).then_inc(shift_ready, 1)

            def add_bo(u):
                if u == B:
                    pool.wait_ge(rows_loaded, 16)
                pool.wait_ge(xn_ready, u + 1)
                pool.wait_ge(xn_act_ready, u + 1)
                bo = ROW[:, BO, :].unsqueeze(1).to_broadcast([P, T, D])
                nc.gpsimd.tensor_tensor(X[:, u % B], X[:, u % B], bo, ALU.add).then_inc(bo_added, 1)

            def sum_kf(u):
                n = atts(u)
                k = kf[u % 2]
                pool.wait_ge(kf_ready, n)
                if n > 2:
                    pool.wait_ge(ksum_ps_ready, n - 2)
                nc.gpsimd.tensor_tensor(kf2[u % 2][:], k[:, 0:T // 2, :], k[:, T // 2:T, :], ALU.add).then_inc(kf2_done, 1)
                pool.wait_ge(kf2_done, n)
                nc.gpsimd.tensor_tensor(kf1[u % 2][:], kf2[u % 2][:, 0, :], kf2[u % 2][:, 1, :],
                                        ALU.add).then_inc(kf1_ready, 1)

            def add_gated(u):
                pool.wait_ge(gated_ready, layers(u))
                nc.gpsimd.tensor_tensor(X[:, u % B], X[:, u % B], gated[u % 2][:], ALU.add).then_inc(x_gated, 1)

            def masks():
                nc.gpsimd.memset(head_mask[:], 1.0).then_inc(pool_step, 1)
                nc.gpsimd.memset(head_of[:], 1.0).then_inc(pool_step, 1)
                pool.wait_ge(pool_step, 4)
                for lo in range(2):
                    base, sign = ((0, 1), (DH - 1, -1))[lo]
                    nc.gpsimd.affine_select(out=head_mask[:], in_=head_mask[:], compare_op=ALU.is_ge, fill=0.0,
                                            base=base, pattern=[[-sign * DH, HEADS], [0, DH]],
                                            channel_multiplier=sign).then_inc(masks_made, 1)
                    nc.gpsimd.affine_select(out=head_of[:], in_=head_of[:], compare_op=ALU.is_ge, fill=0.0,
                                            base=base, pattern=[[-sign * DH, HEADS]],
                                            channel_multiplier=sign).then_inc(masks_made, 1)
                    pool.wait_ge(masks_made, 2 * lo + 2)

            masks()
            for s in STEPS:
                if att(s - 1):
                    sum_kf(s - 1)
                if ffn(s - 2) and s - 2 not in BY_VECTOR:
                    add_gated(s - 2)
                if 0 <= s + 5 < UNITS:
                    rstd_of(s + 5)
                if att(s - 1):
                    add_bo(s - 1)

        @block.scalar
        def _(act):
            act.dma_start(COL[:], columns).then_inc(columns_loaded, 16)
            act.dma_start(W[:], weights.rearrange("(i p) d -> p i d", p=P)).then_inc(weights_loaded, 16)
            act.dma_start(ROW[:], rows.partition_broadcast(P)).then_inc(rows_loaded, 16)

            def normalize(u):
                r, c = u % 4, u % B
                act.wait_ge(shift_ready, u + 1)
                if u >= 4:
                    act.wait_ge(t_ready, u - 3)
                    if att(u - 4):
                        act.wait_ge(gram_ps_ready, atts(u - 4))
                for t in act_tiles(u):
                    last = nc.scalar.activation(xn[r][:, t, :], X[:, c, t, :], ACT.Identity,
                                                bias=shift[r][:, t:t + 1], scale=rstd[r][:, t:t + 1])
                    if t != T - 1:
                        yield
                last.then_inc(xn_act_ready, 1)

            def take_xnT(u):
                act.wait_ge(t_ready, u + 1)
                if att(u):
                    if atts(u) > 3:
                        act.wait_ge(aq_ready, atts(u) - 3)
                    nc.scalar.activation(xnT[u % 3][:], bank_T[u % 2][:], ACT.Copy).then_inc(xnT_ready, 1)
                else:
                    if layers(u) > 2:
                        act.wait_ge(k_ready, layers(u) - 2)
                        act.wait_ge(r_ready, layers(u) - 2)
                    nc.scalar.activation(xkT[u % 2][:], bank_T[u % 2][:], ACT.Copy, scale=COL[:, MU_K:MU_K + 1])
                    nc.scalar.activation(xrT[u % 2][:], bank_T[u % 2][:], ACT.Copy,
                                         scale=COL[:, MU_R:MU_R + 1]).then_inc(mu_x_ready, 1)

            def relu_k(u):
                n = layers(u)
                act.wait_ge(k_ready, n)
                if n > 2:
                    act.wait_ge(kact_ready, n - 2)
                nc.scalar.activation(kpos[u % 2][:], bank_K[u % 2][:], ACT.Relu).then_inc(kpos_done, 1)

            def square_k(u):
                n = layers(u)
                act.wait_ge(kpos_done, n)
                if n > 2:
                    act.wait_ge(v_ready, n - 2)
                nc.scalar.activation(kact[u % 2][:], kpos[u % 2][:], ACT.Square).then_inc(kact_ready, 1)

            def gate_of(u):
                n = layers(u)
                act.wait_ge(r_ready, n)
                if n > 2:
                    act.wait_ge(gated_ready, n - 2)
                nc.scalar.activation(gate[u % 2][:].rearrange("p t d -> p (t d)"), bank_R[u % 2][:], ACT.Tanh,
                                     scale=0.5).then_inc(gate_ready, 1)

            def features_k(u):
                n = atts(u)
                act.wait_ge(ak_ready, n)
                if n > 2:
                    act.wait_ge(kf_ready, n - 2)
                flat = [r[u % 2][:].rearrange("p t d -> p (t d)") for r in (ek, rk)]
                nc.scalar.activation(flat[0], bank_k[:], ACT.Exp)
                nc.scalar.activation(flat[1], bank_k[:], ACT.Relu).then_inc(ek_ready, 1)

            def features_q(u):
                n = atts(u)
                act.wait_ge(aq_ready, n)
                if n > 2:
                    act.wait_ge(qf_ready, n - 2)
                nc.scalar.activation(eq[u % 2][:], bank_q[:], ACT.Exp, bias=COL[:, BQ:BQ + 1])
                nc.scalar.activation(rq[u % 2][:], bank_q[:], ACT.Relu, bias=COL[:, BQ:BQ + 1]).then_inc(eq_ready, 1)

            def widen_z(u):
                n = atts(u)
                act.wait_ge(z_ready, n)
                if n > 2:
                    act.wait_ge(zT_ready, n - 2)
                nc.scalar.activation(z_wide[u % 2][:].rearrange("p t h e -> p (t h) e"),
                                     z[u % 2][:].rearrange("p t h -> p (t h)").unsqueeze(2).to_broadcast([P, T * HEADS, DH]),
                                     ACT.Copy).then_inc(z_wide_ready, 1)

            def take_gram(u):
                n = atts(u)
                act.wait_ge(gram_ps_ready, n)
                nc.scalar.activation(gram[u % 2][:], bank_g[:, 0:D], ACT.Copy).then_inc(gram_ready, 1)

            for s in STEPS:
                if s == -2:
                    act.wait_ge(columns_loaded, 16)
                norm = normalize(s + 3) if 0 <= s + 3 < UNITS else iter(())
                if ffn(s):
                    next(norm, None)
                    relu_k(s)
                    for _ in norm:
                        pass
                    square_k(s)
                    gate_of(s)
                for _ in norm:
                    pass
                if att(s):
                    features_k(s)
                    features_q(s)
                if att(s - 1):
                    widen_z(s - 1)
                if 0 <= s + 2 < UNITS:
                    take_xnT(s + 2)
                if att(s):
                    take_gram(s)

        @block.vector
        def _(dve):
            nc.vector.memset(ones[:], 1.0)
            nc.vector.memset(third[:], 1.0 / 32).then_inc(setup_done, 1)

            def stats_of(u):
                r, c = u % 4, u % B
                if u < B:
                    dve.wait_ge(x_loaded[c], 16)
                elif u < 2 * B:
                    dve.wait_ge(x_gated, c + 1)
                else:
                    dve.wait_ge(x_attended, c + 1)
                if u >= 4:
                    dve.wait_ge(shift_ready, u - 3)
                for t in range(T):
                    last = nc.vector.bn_stats(stats[r][:, t, :], X[:, c, t, :])
                last.then_inc(stats_done, 1)

            def gather_stats(u):
                r = u % 4
                dve.wait_ge(stats_done, u + 1)
                for t in range(T):
                    last = nc.vector.bn_aggr(mean_var[r][:, t, :], stats[r][:, t, :])
                last.then_inc(mean_var_ready, 1)

            def normalize(u):
                r, c = u % 4, u % B
                dve.wait_ge(rstd_ready, u + 1)
                if u >= 4:
                    dve.wait_ge(t_ready, u - 3)
                    if att(u - 4):
                        dve.wait_ge(gram_ps_ready, atts(u - 4))
                for t in range(T):
                    if t in act_tiles(u):
                        continue
                    last = nc.vector.tensor_scalar(xn[r][:, t, :], X[:, c, t, :], mean_var[r][:, t, 0:1],
                                                   rstd[r][:, t:t + 1], ALU.subtract, ALU.mult)
                last.then_inc(xn_ready, 1)

            def mix(u):
                n = layers(u)
                dve.wait_ge(mu_x_ready, n)
                prev = bank_T[u % 2][:, 0:S - 1]
                for mixed, m, ready in ((xkT, MU_K, xk_ready), (xrT, MU_R, xr_ready)):
                    rest = mixed[u % 2][:, 1:S]
                    nc.vector.scalar_tensor_tensor(out=rest, in0=prev, scalar=prev_mu[:, m:m + 1], in1=rest,
                                                   op0=ALU.mult, op1=ALU.add).then_inc(ready, 1)

            def gate_values(u):
                n = layers(u)
                dve.wait_ge(v_ready, n)
                dve.wait_ge(gate_ready, n)
                if n > 2:
                    dve.wait_ge(x_gated, n - 2)
                nc.vector.scalar_tensor_tensor(out=gated[u % 2][:].rearrange("p t d -> p (t d)"),
                                               in0=gate[u % 2][:].rearrange("p t d -> p (t d)"), scalar=1.0,
                                               in1=bank_V[u % 2][:], op0=ALU.add, op1=ALU.mult).then_inc(gated_ready, 1)

            def features_k(u):
                n = atts(u)
                dve.wait_ge(ek_ready, n)
                if n > 2:
                    dve.wait_ge(gram_ps_ready, n - 2)
                    dve.wait_ge(kf2_done, n - 2)
                nc.vector.scalar_tensor_tensor(out=kf[u % 2][:], in0=ek[u % 2][:], scalar=1.0, in1=rk[u % 2][:],
                                               op0=ALU.min, op1=ALU.add).then_inc(kf_ready, 1)

            def features_q(u):
                n = atts(u)
                dve.wait_ge(eq_ready, n)
                nc.vector.scalar_tensor_tensor(out=qfT[u % 2][:], in0=eq[u % 2][:], scalar=1.0, in1=rq[u % 2][:],
                                               op0=ALU.min, op1=ALU.add).then_inc(qf_ready, 1)

            def spread_ksum(u):
                n = atts(u)
                dve.wait_ge(ksum_ps_ready, n)
                nc.vector.tensor_copy(ksum[u % 2][:], bank_d[:, 0:1])
                nc.vector.tensor_scalar(ksum_head[u % 2][:], head_of[:], bank_d[:, 0:1], None,
                                        ALU.mult).then_inc(ksum_ready, 1)

            def take_kvo(u):
                n = atts(u)
                dve.wait_ge(kvo_ps_ready, n)
                dve.wait_ge(ksum_ready, n)
                nc.vector.scalar_tensor_tensor(out=kvo[u % 2][:], in0=bv_wo[:], scalar=ksum[u % 2][:], in1=bank_g[:, 0:D],
                                               op0=ALU.mult, op1=ALU.add).then_inc(kvo_ready, 1)

            def mask_kv(u):
                n = atts(u)
                dve.wait_ge(kvT_ps_ready, n)
                nc.vector.tensor_tensor(kvT[u % 2][:], bank_g[:, 0:D], head_mask[:].rearrange("p h e -> p (h e)"),
                                        ALU.mult).then_inc(kvT_ready, 1)

            def z_of(u):
                n = atts(u)
                dve.wait_ge(den_ps_ready, n)
                nc.vector.tensor_scalar(den[u % 2][:].rearrange("p t h -> p (t h)"), bank_d[:, 64:64 + T * HEADS],
                                        DEN_EPS, None, ALU.add).then_inc(den_done, 1)
                dve.wait_ge(den_done, n)
                nc.vector.reciprocal(z[u % 2][:], den[u % 2][:]).then_inc(z_ready, 1)

            def scale_q(u):
                n = atts(u)
                dve.wait_ge(zT_ready, n)
                nc.vector.tensor_tensor(qzT[u % 2][:], qfT[u % 2][:], bank_z[:], ALU.mult).then_inc(qz_ready, 1)

            def add_attended(u):
                n = atts(u)
                dve.wait_ge(o_ready, n)
                dve.wait_ge(bo_added, n)
                xc = X[:, u % B].rearrange("p t d -> p (t d)")
                nc.vector.tensor_tensor(xc, xc, bank_o[:], ALU.add).then_inc(x_attended, 1)

            def split_bk():
                dve.wait_ge(rows_loaded, 16)
                a, b, rest, rest2 = part
                R = ROW[:, BK, :]
                nc.vector.tensor_copy(a[:], R).then_inc(bias_step, 1)
                dve.wait_ge(bias_step, 1)
                nc.vector.tensor_tensor(rest[:], R, a[:], ALU.subtract).then_inc(bias_step, 1)
                dve.wait_ge(bias_step, 2)
                nc.vector.tensor_copy(b[:], rest[:]).then_inc(bias_step, 1)
                dve.wait_ge(bias_step, 3)
                nc.vector.tensor_tensor(rest2[:], rest[:], b[:], ALU.subtract).then_inc(bias_step, 1)
                dve.wait_ge(bias_step, 4)
                for q, p in enumerate((a, b, rest2)):
                    rows32 = slice(32 * q, 32 * q + 32)
                    nc.vector.tensor_copy(bias_k[rows32], p[rows32].unsqueeze(1).to_broadcast([32, T, D]))
                nc.vector.memset(bias_k[96:128], 0.0).then_inc(bias_ready, 1)

            def add_gated(u):
                dve.wait_ge(gated_ready, layers(u))
                c = u % B
                nc.vector.tensor_tensor(X[:, c], X[:, c], gated[u % 2][:], ALU.add).then_inc(x_gated_last, 1)

            def next_norms(s):
                if 0 <= s + 5 < UNITS:
                    stats_of(s + 5)
                if 0 <= s + 3 < UNITS:
                    normalize(s + 3)
                if 0 <= s + 5 < UNITS:
                    gather_stats(s + 5)

            for s in STEPS:
                if s == -1:
                    dve.wait_ge(columns_loaded, 16)
                    nc.vector.tensor_scalar(prev_mu[:], COL[:, 0:2], -1.0, 1.0, ALU.mult, ALU.add).then_inc(setup_done, 1)
                if s == 0:
                    dve.wait_ge(weights_loaded, 16)
                    nc.vector.tensor_scalar(Wv4[:], W[:, W_V, :], 0.25, None, ALU.mult).then_inc(setup_done, 1)
                if s == 2:
                    split_bk()
                if s == 1:
                    dve.wait_ge(masks_made, 4)
                    nc.vector.tensor_scalar(bv_heads[:], head_mask[:].rearrange("p h e -> p (h e)"), COL[:, BV:BV + 1],
                                            None, ALU.mult).then_inc(setup_done, 1)
                if s == 3:
                    dve.wait_ge(bv_wo_ps_ready, 1)
                    nc.vector.tensor_copy(bv_wo[:], bank[6][:, 0:D]).then_inc(bv_wo_ready, 1)
                if att(s - 2):
                    scale_q(s - 2)
                if att(s - 1):
                    mask_kv(s - 1)
                if s < 0:
                    if s == -1:
                        dve.wait_ge(setup_done, 2)
                        normalize(2)
                        mix(0)
                        stats_of(4)
                        gather_stats(4)
                    else:
                        if s + 4 >= 0:
                            normalize(s + 3) if s + 3 >= 0 else None
                        stats_of(s + 5)
                        gather_stats(s + 5)
                    continue
                if ffn(s + 1) and not att(s) and not att(s - 1):
                    mix(s + 1)
                if att(s):
                    next_norms(s)
                if att(s - 1):
                    spread_ksum(s - 1)
                    take_kvo(s - 1)
                if ffn(s + 1) and not att(s) and att(s - 1):
                    mix(s + 1)
                if not att(s):
                    next_norms(s)
                if att(s):
                    features_k(s)
                if att(s - 1):
                    z_of(s - 1)
                if att(s):
                    features_q(s)
                if att(s - 2):
                    add_attended(s - 2)
                if ffn(s + 1) and att(s):
                    mix(s + 1)
                if ffn(s - 1):
                    gate_values(s - 1)
                if s - 1 in BY_VECTOR:
                    add_gated(s - 1)

        @block.tensor
        def _(pe):
            def transpose_x(u):
                pe.wait_ge(xn_ready, u + 1)
                pe.wait_ge(xn_act_ready, u + 1)
                if u >= 2:
                    if ffn(u - 2):
                        pe.wait_ge(xr_ready, layers(u - 2))
                    else:
                        pe.wait_ge(xnT_ready, atts(u - 2))
                for t in range(T):
                    last = nc.tensor.transpose(bank_T[u % 2][:, t * P:(t + 1) * P], xn[u % 4][:, t, :], ident[:])
                last.then_inc(t_ready, 1)

            def ffn_k(u):
                n = layers(u)
                pe.wait_ge(xk_ready, n)
                if n > 2:
                    pe.wait_ge(kpos_done, n - 2)
                if u == 2 * B:
                    pe.wait_ge(ek_ready, B)
                if u == 2 * B + 1:
                    pe.wait_ge(kvo_ready, B)
                nc.tensor.matmul(bank_K[u % 2][:], W[:, W_K, :], xkT[u % 2][:], start=True, stop=True).then_inc(k_ready, 1)

            def ffn_r(u):
                n = layers(u)
                pe.wait_ge(xr_ready, n)
                if n > 2:
                    pe.wait_ge(gate_ready, n - 2)
                if u == 2 * B:
                    pe.wait_ge(eq_ready, B)
                if u == 2 * B + 1:
                    pe.wait_ge(qz_ready, B)
                for t in range(T):
                    last = nc.tensor.matmul(bank_R[u % 2][:, t * P:(t + 1) * P], xrT[u % 2][:, t * P:(t + 1) * P],
                                            W[:, W_R, :], start=True, stop=True)
                last.then_inc(r_ready, 1)

            def ffn_v(u):
                n = layers(u)
                pe.wait_ge(kact_ready, n)
                if n > 2:
                    pe.wait_ge(gated_ready, n - 2)
                if u == 2 * B:
                    pe.wait_ge(den_done, B)
                if u == 0:
                    pe.wait_ge(setup_done, 3)
                if u == 2:
                    pe.wait_ge(bv_wo_ready, 1)
                if u == 2 * B + 1:
                    pe.wait_ge(x_attended, B)
                for t in range(T):
                    last = nc.tensor.matmul(bank_V[u % 2][:, t * P:(t + 1) * P], kact[u % 2][:, t * P:(t + 1) * P],
                                            Wv4[:], start=True, stop=True)
                last.then_inc(v_ready, 1)

            def att_k(u):
                n = atts(u)
                pe.wait_ge(xnT_ready, n)
                if n == 1:
                    pe.wait_ge(bias_ready, 1)
                    pe.wait_ge(kpos_done, B - 1)
                if n > 1:
                    pe.wait_ge(ek_ready, n - 1)
                nc.tensor.matmul(bank_k[:], third[:], bias_k[:].rearrange("p t d -> p (t d)"), start=True, stop=False)
                for t in range(T):
                    last = nc.tensor.matmul(bank_k[:, t * P:(t + 1) * P], xnT[u % 3][:, t * P:(t + 1) * P],
                                            W[:, WK, :], start=False, stop=(t == T - 1))
                last.then_inc(ak_ready, 1)

            def att_q(u):
                n = atts(u)
                if n == 1:
                    pe.wait_ge(gate_ready, B - 1)
                if n > 1:
                    pe.wait_ge(eq_ready, n - 1)
                nc.tensor.matmul(bank_q[:], W[:, WQ, :], xnT[u % 3][:], start=True, stop=True).then_inc(aq_ready, 1)

            def att_gram(u):
                n = atts(u)
                pe.wait_ge(kf_ready, n)
                if n == 1:
                    pe.wait_ge(kpos_done, B)
                if n > 1:
                    pe.wait_ge(kvo_ready, n - 1)
                for t in range(T):
                    last = nc.tensor.matmul(bank_g[:, 0:D], xn[u % 4][:, t, :], kf[u % 2][:, t, :],
                                            start=(t == 0), stop=(t == T - 1))
                last.then_inc(gram_ps_ready, 1)

            def att_ksum(u):
                n = atts(u)
                pe.wait_ge(kf1_ready, n)
                if n == 1:
                    pe.wait_ge(gated_ready, B - 1)
                if n > 1:
                    pe.wait_ge(den_done, n - 1)
                nc.tensor.matmul(bank_d[:, 0:1], kf1[u % 2][:], ones[:], start=True, stop=True).then_inc(ksum_ps_ready, 1)

            def att_kv(u):
                n = atts(u)
                pe.wait_ge(gram_ready, n)
                nc.tensor.matmul(bank_g[:, 0:D], W[:, WV, :], gram[u % 2][:], start=True, stop=True).then_inc(kvT_ps_ready, 1)

            def att_den(u):
                n = atts(u)
                pe.wait_ge(qf_ready, n)
                pe.wait_ge(ksum_ready, n)
                for t in range(T):
                    last = nc.tensor.matmul(bank_d[:, 64 + t * HEADS:64 + (t + 1) * HEADS],
                                            qfT[u % 2][:, t * P:(t + 1) * P], ksum_head[u % 2][:], start=True, stop=True)
                last.then_inc(den_ps_ready, 1)

            def att_z(u):
                n = atts(u)
                pe.wait_ge(z_wide_ready, n)
                if n == 1:
                    pe.wait_ge(gate_ready, B)
                if n > 1:
                    pe.wait_ge(qz_ready, n - 1)
                for t in range(T):
                    last = nc.tensor.transpose(bank_z[:, t * P:(t + 1) * P],
                                               z_wide[u % 2][:, t].rearrange("p h e -> p (h e)"), ident[:])
                last.then_inc(zT_ready, 1)

            def att_kvo(u):
                n = atts(u)
                pe.wait_ge(kvT_ready, n)
                nc.tensor.matmul(bank_g[:, 0:D], kvT[u % 2][:], W[:, WO, :], start=True, stop=True).then_inc(kvo_ps_ready, 1)

            def att_out(u):
                n = atts(u)
                pe.wait_ge(kvo_ready, n)
                pe.wait_ge(qz_ready, n)
                if n == 1:
                    pe.wait_ge(gated_ready, B)
                if n > 1:
                    pe.wait_ge(x_attended, n - 1)
                for t in range(T):
                    last = nc.tensor.matmul(bank_o[:, t * P:(t + 1) * P], qzT[u % 2][:, t * P:(t + 1) * P],
                                            kvo[u % 2][:], start=True, stop=True)
                last.then_inc(o_ready, 1)

            def keep_warm(n):
                for _ in range(n):
                    nc.tensor.matmul(bank[7][:, 0:P], third[:], third[:], start=True, stop=True)

            pe.wait_ge(setup_done, 1)
            keep_warm(WARM[0])
            pe.wait_ge(id_made, 1)
            for s in STEPS:
                if s == 0:
                    pe.wait_ge(weights_loaded, 16)
                if s == 2:
                    pe.wait_ge(setup_done, 4)
                    pe.wait_ge(gated_ready, 1)
                    nc.tensor.matmul(bank[6][:, 0:D], bv_heads[:], W[:, WO, :], start=True, stop=True).then_inc(bv_wo_ps_ready, 1)
                if att(s - 1):
                    att_kv(s - 1)
                if ffn(s):
                    ffn_k(s)
                    ffn_r(s)
                if att(s):
                    att_k(s)
                if att(s - 1):
                    att_ksum(s - 1)
                    att_kvo(s - 1)
                if att(s):
                    att_q(s)
                if att(s - 1):
                    att_den(s - 1)
                if att(s - 2):
                    att_out(s - 2)
                if 0 <= s + 2 < UNITS:
                    transpose_x(s + 2)
                    if s < 0:
                        keep_warm(WARM[s])
                if ffn(s - 1):
                    ffn_v(s - 1)
                if att(s):
                    att_gram(s)
                if att(s - 1):
                    att_z(s - 1)


def kernel(**inputs):
    import concourse.bacc as bacc
    from concourse.bass_utils import run_bass_kernel_spmd as run

    given = {k: np.ascontiguousarray(v) for k, v in inputs.items()}
    arrays = {
        "x": given["L0_attn_x"],
        "weights": np.concatenate([given[f"L0_ffn_{n}"].T for n in ("W_r", "W_k", "W_v")]
                                  + [given[f"L0_attn_{n}"] for n in ("wq", "wk", "wv", "wo")], axis=0),
        "columns": np.stack([given["L0_ffn_mu_r"], given["L0_ffn_mu_k"], given["L0_attn_bq"], given["L0_attn_bv"]],
                            axis=1),
        "rows": np.stack([given["L0_attn_bk"], given["L0_attn_bo"]], axis=0),
    }
    arrays = {k: np.ascontiguousarray(v) for k, v in arrays.items()}
    nc = bacc.Bacc("TRN2", target_bir_lowering=False, num_devices=1)
    args = [nc.dram_tensor(k, v.shape, mybir.dt.from_np(v.dtype), kind="ExternalInput").ap() for k, v in arrays.items()]
    out = nc.dram_tensor("out", arrays["x"].shape, mybir.dt.float32, kind="ExternalOutput").ap()
    macaron_block(nc, *args, out)
    r = run(nc, [arrays], core_ids=[0])
    return r.results[0]["out"]
```

```python
import numpy as np
import concourse.bass as bass
from concourse import mybir
from contextlib import ExitStack

W_R, W_K, W_V, WQ, WK, WV, WO = range(7)
MU_R, MU_K, BQ, BV = range(4)
BK, BO = range(2)
HEADS = 16
LN_EPS = 1e-5
DEN_EPS = 1e-6


def macaron_block(nc: bass.Bass, x: bass.AP, weights: bass.AP, columns: bass.AP, rows: bass.AP, out: bass.AP):
    fp32 = mybir.dt.float32
    bf16 = mybir.dt.bfloat16
    ALU = mybir.AluOpType
    ACT = mybir.ActivationFunctionType

    B, S, D = x.shape
    P = 128
    T = S // P
    DH = D // HEADS
    assert D == P and S == 512 and B == 8
    UNITS = 3 * B
    LAST = UNITS - 1
    POOLED = (1, 10)

    def ffn(u):
        return 0 <= u < B or 2 * B <= u < UNITS

    def att(u):
        return B <= u < 2 * B

    def layers(u):
        return u + 1 if u < B else B if u < 2 * B else u + 1 - B

    def atts(u):
        return min(max(u + 1 - B, 0), B)

    def of(kind):
        return lambda stage: lambda u, *rest: stage(u, *rest) if kind(u) else None

    def unit(u):
        return 0 <= u < UNITS

    def first_act_tile(u):
        return 3 if u >= 22 else 1 if u >= 14 else 2

    def pooled(u):
        return min(max(u + 1 - POOLED[0], 0), POOLED[1] - POOLED[0])

    ctx = ExitStack()
    with ctx:
        def sb(name, shape, dt=fp32):
            return ctx.enter_context(nc.sbuf_tensor(name, shape, dt))

        def sem(name):
            return ctx.enter_context(nc.semaphore(name))

        X = sb("X", [P, B, T, D])
        W = sb("W", [P, 7, D])
        Wv4 = sb("Wv4", [P, D])
        COL = sb("COL", [P, 4])
        ROW = sb("ROW", [P, 2, D])
        prev_mu = sb("prev_mu", [P, 2])
        bv_heads = sb("bv_heads", [P, D])
        bv_wo = sb("bv_wo", [P, D])
        ident = sb("ident", [P, P])
        head_mask = sb("head_mask", [P, HEADS, DH])
        head_of = sb("head_of", [P, HEADS])
        ones = sb("ones", [P, 1])
        minus_half = sb("minus_half", [P, T])
        third = sb("third", [P, P], bf16)
        bias_k = sb("bias_k", [P, D], bf16)
        part = [sb(f"part{n}", [P, D], bf16 if n < 2 else fp32) for n in range(4)]

        def ring(name, n, shape):
            return [sb(f"{name}{i}", shape) for i in range(n)]

        stats = ring("stats", 4, [P, T, nc.vector.BN_STATS_DIM])
        mean_var = ring("mean_var", 4, [P, T, nc.vector.BN_AGGR_DIM])
        var_eps = ring("var_eps", 4, [P, T])
        rstd = ring("rstd", 4, [P, T])
        neg_mean = ring("neg_mean", 4, [P, T])
        shift = ring("shift", 4, [P, T])
        xn = ring("xn", 4, [P, T, D])
        xnT = ring("xnT", 3, [P, S])
        xkT = ring("xkT", 2, [P, S])
        xrT = ring("xrT", 2, [P, S])
        kpos = ring("kpos", 2, [P, S])
        kact = ring("kact", 2, [P, S])
        gate = ring("gate", 2, [P, T, D])
        gated = ring("gated", 2, [P, T, D])
        ek = ring("ek", 2, [P, T, D])
        rk = ring("rk", 2, [P, T, D])
        kf = ring("kf", 2, [P, T, D])
        eq = ring("eq", 2, [P, S])
        rq = ring("rq", 2, [P, S])
        qfT = ring("qfT", 2, [P, S])
        gram = ring("gram", 2, [P, D])
        kf2 = ring("kf2", 2, [P, T // 2, D])
        kf1 = ring("kf1", 2, [P, D])
        ksum = ring("ksum", 2, [P, 1])
        ksum_head = ring("ksum_head", 2, [P, HEADS])
        kvT = ring("kvT", 2, [P, D])
        kvo = ring("kvo", 2, [P, D])
        den = ring("den", 2, [P, T, HEADS])
        z = ring("z", 2, [P, T, HEADS])
        z_wide = ring("z_wide", 2, [P, T, HEADS, DH])
        qzT = ring("qzT", 2, [P, S])

        bank = [ctx.enter_context(nc.psum_tensor(f"bank{i}", [P, 512], fp32)) for i in range(8)]
        bank_T = bank[0:2]
        bank_K, bank_R, bank_V = bank[2:4], bank[4:6], bank[6:8]
        bank_V2 = bank_K[(LAST - 1) % 2]
        bank_k, bank_q, bank_d = bank[2], bank[4], bank[6]
        bank_g, bank_z, bank_o = bank[3], bank[5], bank[7]

        x_loaded = [sem(f"x_loaded{c}") for c in range(B)]
        columns_loaded = sem("columns_loaded")
        weights_loaded = sem("weights_loaded")
        rows_loaded = sem("rows_loaded")
        last_gated = sem("last_gated")
        id_made = sem("id_made")
        masks_made = sem("masks_made")
        pool_step = sem("pool_step")
        bias_ready = sem("bias_ready")
        bias_step = sem("bias_step")
        setup_done = sem("setup_done")
        stats_done = sem("stats_done")
        mean_var_ready = sem("mean_var_ready")
        var_eps_done = sem("var_eps_done")
        rstd_ready = sem("rstd_ready")
        xn_ready = sem("xn_ready")
        t_ready = sem("t_ready")
        xnT_ready = sem("xnT_ready")
        mu_x_ready = sem("mu_x_ready")
        shift_ready = sem("shift_ready")
        xn_act_ready = sem("xn_act_ready")
        xn_pool_ready = sem("xn_pool_ready")
        bo_added = sem("bo_added")
        kf2_done = sem("kf2_done")
        kf1_ready = sem("kf1_ready")
        bv_wo_ps_ready = sem("bv_wo_ps_ready")
        bv_wo_ready = sem("bv_wo_ready")
        xk_ready = sem("xk_ready")
        xr_ready = sem("xr_ready")
        k_ready = sem("k_ready")
        r_ready = sem("r_ready")
        kpos_done = sem("kpos_done")
        kact_ready = sem("kact_ready")
        gate_ready = sem("gate_ready")
        v_ready = sem("v_ready")
        gated_ready = sem("gated_ready")
        x_gated = sem("x_gated")
        ak_ready = sem("ak_ready")
        aq_ready = sem("aq_ready")
        ek_ready = sem("ek_ready")
        eq_ready = sem("eq_ready")
        kf_ready = sem("kf_ready")
        qf_ready = sem("qf_ready")
        gram_ps_ready = sem("gram_ps_ready")
        ksum_ps_ready = sem("ksum_ps_ready")
        gram_ready = sem("gram_ready")
        ksum_ready = sem("ksum_ready")
        kvT_ps_ready = sem("kvT_ps_ready")
        kvT_ready = sem("kvT_ready")
        den_ps_ready = sem("den_ps_ready")
        den_done = sem("den_done")
        z_ready = sem("z_ready")
        z_wide_ready = sem("z_wide_ready")
        zT_ready = sem("zT_ready")
        kvo_ps_ready = sem("kvo_ps_ready")
        kvo_ready = sem("kvo_ready")
        qz_ready = sem("qz_ready")
        o_ready = sem("o_ready")
        x_attended = sem("x_attended")
        stored = sem("stored")

        block = ctx.enter_context(nc.Block())

        def tiles(ap):
            return ap.rearrange("(t p) d -> p t d", p=P)

        @block.sync
        def _(sp):
            for c in range(B):
                sp.dma_start(X[:, c], tiles(x[c])).then_inc(x_loaded[c], 16)
            for c in range(B - 1):
                sp.wait_ge(x_gated, B + c + 1)
                sp.dma_start(tiles(out[c]), X[:, c]).then_inc(stored, 16)
            for h in range(2):
                ts = slice(h * T // 2, (h + 1) * T // 2)
                sp.wait_ge(last_gated, h + 1)
                sp.dma_start(tiles(out[B - 1])[:, ts, :], X[:, B - 1, ts, :]).then_inc(stored, 16)
            sp.wait_ge(stored, 16 * (B + 1))

        @block.gpsimd
        def _(pool):
            nc.gpsimd.memset(ident[:], 0.0).then_inc(pool_step, 1)
            nc.gpsimd.memset(minus_half[:], -0.5).then_inc(pool_step, 1)
            pool.wait_ge(pool_step, 2)
            nc.gpsimd.affine_select(out=ident[:], in_=ident[:], compare_op=ALU.not_equal, fill=1.0, base=0,
                                    pattern=[[-1, P]], channel_multiplier=1).then_inc(id_made, 1)

            @of(unit)
            def rstd_of(u):
                r = u % 4
                pool.wait_ge(mean_var_ready, u + 1)
                if u >= 4:
                    pool.wait_ge(xn_act_ready, u - 3)
                nc.gpsimd.tensor_scalar(var_eps[r][:], mean_var[r][:, :, 1], 1.0, LN_EPS, ALU.mult,
                                        ALU.add).then_inc(var_eps_done, 1)
                nc.gpsimd.tensor_scalar(neg_mean[r][:], mean_var[r][:, :, 0], -1.0, 0.0, ALU.mult, ALU.add)
                pool.wait_ge(var_eps_done, u + 1)
                nc.gpsimd.tensor_tensor(rstd[r][:], var_eps[r][:], minus_half[:], ALU.pow).then_inc(rstd_ready, 1)
                pool.wait_ge(rstd_ready, u + 1)
                nc.gpsimd.tensor_tensor(shift[r][:], neg_mean[r][:], rstd[r][:], ALU.mult).then_inc(shift_ready, 1)

            @of(lambda u: pooled(u) > pooled(u - 1))
            def normalize(u):
                r, c = u % 4, u % B
                pool.wait_ge(shift_ready, u + 1)
                if u >= 4:
                    pool.wait_ge(t_ready, u - 3)
                    if att(u - 4):
                        pool.wait_ge(gram_ps_ready, atts(u - 4))
                nc.gpsimd.tensor_scalar(xn[r][:, 0, :], X[:, c, 0, :], rstd[r][:, 0:1], shift[r][:, 0:1],
                                        ALU.mult, ALU.add).then_inc(xn_pool_ready, 1)

            @of(att)
            def add_bo(u):
                if u == B:
                    pool.wait_ge(rows_loaded, 16)
                pool.wait_ge(xn_ready, u + 1)
                pool.wait_ge(xn_act_ready, u + 1)
                bo = ROW[:, BO, :].unsqueeze(1).to_broadcast([P, T, D])
                nc.gpsimd.tensor_tensor(X[:, u % B], X[:, u % B], bo, ALU.add).then_inc(bo_added, 1)

            @of(att)
            def sum_kf(u):
                n = atts(u)
                k = kf[u % 2]
                pool.wait_ge(kf_ready, n)
                if n > 2:
                    pool.wait_ge(ksum_ps_ready, n - 2)
                nc.gpsimd.tensor_tensor(kf2[u % 2][:], k[:, 0:T // 2, :], k[:, T // 2:T, :],
                                        ALU.add).then_inc(kf2_done, 1)
                pool.wait_ge(kf2_done, n)
                nc.gpsimd.tensor_tensor(kf1[u % 2][:], kf2[u % 2][:, 0, :], kf2[u % 2][:, 1, :],
                                        ALU.add).then_inc(kf1_ready, 1)

            @of(lambda u: ffn(u) and u != LAST)
            def add_gated(u):
                pool.wait_ge(gated_ready, layers(u))
                nc.gpsimd.tensor_tensor(X[:, u % B], X[:, u % B], gated[u % 2][:], ALU.add).then_inc(x_gated, 1)

            def split_bk():
                pool.wait_ge(rows_loaded, 16)
                a, b, rest, rest2 = part
                R = ROW[:, BK, :]
                nc.gpsimd.tensor_copy(a[:], R).then_inc(bias_step, 1)
                pool.wait_ge(bias_step, 1)
                nc.gpsimd.tensor_tensor(rest[:], R, a[:], ALU.subtract).then_inc(bias_step, 1)
                pool.wait_ge(bias_step, 2)
                nc.gpsimd.tensor_copy(b[:], rest[:]).then_inc(bias_step, 1)
                pool.wait_ge(bias_step, 3)
                nc.gpsimd.tensor_tensor(rest2[:], rest[:], b[:], ALU.subtract).then_inc(bias_step, 1)

            def masks():
                nc.gpsimd.memset(head_mask[:], 1.0).then_inc(pool_step, 1)
                nc.gpsimd.memset(head_of[:], 1.0).then_inc(pool_step, 1)
                pool.wait_ge(pool_step, 4)
                for lo in range(2):
                    base, sign = ((0, 1), (DH - 1, -1))[lo]
                    nc.gpsimd.affine_select(out=head_mask[:], in_=head_mask[:], compare_op=ALU.is_ge, fill=0.0,
                                            base=base, pattern=[[-sign * DH, HEADS], [0, DH]],
                                            channel_multiplier=sign).then_inc(masks_made, 1)
                    nc.gpsimd.affine_select(out=head_of[:], in_=head_of[:], compare_op=ALU.is_ge, fill=0.0,
                                            base=base, pattern=[[-sign * DH, HEADS]],
                                            channel_multiplier=sign).then_inc(masks_made, 1)
                    pool.wait_ge(masks_made, 2 * lo + 2)

            masks()
            rstd_of(0)
            rstd_of(1)
            normalize(1)
            rstd_of(2)
            rstd_of(3)
            normalize(2)
            normalize(3)
            rstd_of(4)
            split_bk()
            normalize(4)
            rstd_of(5)
            for s in range(2, B):
                normalize(s + 3)
                add_gated(s - 2)
                rstd_of(s + 4)
            add_gated(6)
            sum_kf(8)
            for s in range(B, 2 * B):
                add_gated(s - 1)
                rstd_of(s + 4)
                add_bo(s - 1)
                sum_kf(s + 1)
            rstd_of(20)
            add_bo(15)
            add_gated(16)
            rstd_of(21)
            rstd_of(22)
            rstd_of(23)
            for s in range(2 * B + 2, UNITS - 2):
                add_gated(s - 1)
            add_gated(21)
            add_gated(22)

        @block.scalar
        def _(act):
            act.dma_start(COL[:], columns).then_inc(columns_loaded, 16)
            act.dma_start(W[:], weights.rearrange("(i p) d -> p i d", p=P)).then_inc(weights_loaded, 16)
            act.dma_start(ROW[:], rows.partition_broadcast(P)).then_inc(rows_loaded, 16)

            @of(unit)
            def normalize(u, n):
                r, c, mine = u % 4, u % B, range(first_act_tile(u), T)
                if n >= len(mine):
                    return
                if n == 0:
                    act.wait_ge(shift_ready, u + 1)
                    if u >= 4:
                        act.wait_ge(t_ready, u - 3)
                        if att(u - 4):
                            act.wait_ge(gram_ps_ready, atts(u - 4))
                t = mine[n]
                done = nc.scalar.activation(xn[r][:, t, :], X[:, c, t, :], ACT.Identity,
                                            bias=shift[r][:, t:t + 1], scale=rstd[r][:, t:t + 1])
                if t == T - 1:
                    done.then_inc(xn_act_ready, 1)

            @of(unit)
            def take_xnT(u):
                act.wait_ge(t_ready, u + 1)
                if att(u):
                    if atts(u) > 3:
                        act.wait_ge(aq_ready, atts(u) - 3)
                    nc.scalar.activation(xnT[u % 3][:], bank_T[u % 2][:], ACT.Copy).then_inc(xnT_ready, 1)
                else:
                    if u == 0:
                        act.wait_ge(columns_loaded, 16)
                    if layers(u) > 2:
                        act.wait_ge(k_ready, layers(u) - 2)
                        act.wait_ge(r_ready, layers(u) - 2)
                    nc.scalar.activation(xkT[u % 2][:], bank_T[u % 2][:], ACT.Copy, scale=COL[:, MU_K:MU_K + 1])
                    nc.scalar.activation(xrT[u % 2][:], bank_T[u % 2][:], ACT.Copy,
                                         scale=COL[:, MU_R:MU_R + 1]).then_inc(mu_x_ready, 1)

            @of(ffn)
            def relu_k(u):
                n = layers(u)
                act.wait_ge(k_ready, n)
                if n > 2:
                    act.wait_ge(kact_ready, n - 2)
                nc.scalar.activation(kpos[u % 2][:], bank_K[u % 2][:], ACT.Relu).then_inc(kpos_done, 1)

            @of(ffn)
            def square_k(u):
                n = layers(u)
                act.wait_ge(kpos_done, n)
                if n > 2:
                    act.wait_ge(v_ready, n - 2)
                nc.scalar.activation(kact[u % 2][:], kpos[u % 2][:], ACT.Square).then_inc(kact_ready, 1)

            @of(ffn)
            def gate_of(u):
                n = layers(u)
                act.wait_ge(r_ready, n)
                if n > 2:
                    act.wait_ge(gated_ready, n - 2)
                nc.scalar.activation(gate[u % 2][:].rearrange("p t d -> p (t d)"), bank_R[u % 2][:], ACT.Tanh,
                                     scale=0.5).then_inc(gate_ready, 1)

            @of(att)
            def features_k(u):
                n = atts(u)
                act.wait_ge(ak_ready, n)
                if n > 2:
                    act.wait_ge(kf_ready, n - 2)
                flat = [r[u % 2][:].rearrange("p t d -> p (t d)") for r in (ek, rk)]
                nc.scalar.activation(flat[0], bank_k[:], ACT.Exp)
                nc.scalar.activation(flat[1], bank_k[:], ACT.Relu).then_inc(ek_ready, 1)

            @of(att)
            def features_q(u):
                n = atts(u)
                act.wait_ge(aq_ready, n)
                if n > 2:
                    act.wait_ge(qf_ready, n - 2)
                nc.scalar.activation(eq[u % 2][:], bank_q[:], ACT.Exp, bias=COL[:, BQ:BQ + 1])
                nc.scalar.activation(rq[u % 2][:], bank_q[:], ACT.Relu, bias=COL[:, BQ:BQ + 1]).then_inc(eq_ready, 1)

            @of(att)
            def widen_z(u):
                n = atts(u)
                act.wait_ge(z_ready, n)
                if n > 2:
                    act.wait_ge(zT_ready, n - 2)
                one_a_head = z[u % 2][:].rearrange("p t h -> p (t h)").unsqueeze(2)
                nc.scalar.activation(z_wide[u % 2][:].rearrange("p t h e -> p (t h) e"),
                                     one_a_head.to_broadcast([P, T * HEADS, DH]),
                                     ACT.Copy).then_inc(z_wide_ready, 1)

            @of(att)
            def take_gram(u):
                n = atts(u)
                act.wait_ge(gram_ps_ready, n)
                nc.scalar.activation(gram[u % 2][:], bank_g[:, 0:D], ACT.Copy).then_inc(gram_ready, 1)

            normalize(0, 0)
            normalize(0, 1)
            normalize(1, 0)
            take_xnT(0)
            normalize(1, 1)
            normalize(2, 0)
            normalize(2, 1)
            take_xnT(1)
            normalize(3, 0)
            gate_of(0)
            take_xnT(2)
            relu_k(0)
            normalize(3, 1)
            normalize(4, 0)
            square_k(0)
            relu_k(1)
            take_xnT(3)
            normalize(4, 1)
            for s in range(2, B):
                square_k(s - 1)
                gate_of(s - 1)
                relu_k(s)
                normalize(s + 3, 0)
                normalize(s + 3, 1)
                take_xnT(s + 2)
            square_k(7)
            features_k(8)
            gate_of(7)
            for s in range(B, 2 * B):
                features_q(s)
                widen_z(s - 1)
                normalize(s + 3, 0)
                take_xnT(s + 2)
                take_gram(s)
                normalize(s + 3, 1)
                features_k(s + 1)
                normalize(s + 3, 2)
            normalize(19, 0)
            relu_k(16)
            square_k(16)
            normalize(20, 0)
            gate_of(16)
            normalize(19, 1)
            normalize(19, 2)
            widen_z(15)
            take_xnT(18)
            normalize(20, 1)
            relu_k(17)
            square_k(17)
            gate_of(17)
            normalize(20, 2)
            take_xnT(19)
            for s in range(2 * B + 2, UNITS - 2):
                normalize(s + 3, 0)
                normalize(s + 3, 1)
                relu_k(s)
                take_xnT(s + 2)
                normalize(s + 3, 2)
                square_k(s)
                gate_of(s)
            relu_k(22)
            square_k(22)
            gate_of(22)
            relu_k(23)
            square_k(23)
            gate_of(23)

        @block.vector
        def _(dve):
            nc.vector.memset(ones[:], 1.0)
            nc.vector.memset(third[:], 1.0 / 32).then_inc(setup_done, 1)

            @of(unit)
            def stats_of(u):
                r, c = u % 4, u % B
                if u < B:
                    dve.wait_ge(x_loaded[c], 16)
                elif u < 2 * B:
                    dve.wait_ge(x_gated, c + 1)
                else:
                    dve.wait_ge(x_attended, c + 1)
                if u >= 4:
                    dve.wait_ge(shift_ready, u - 3)
                for t in range(T):
                    last = nc.vector.bn_stats(stats[r][:, t, :], X[:, c, t, :])
                last.then_inc(stats_done, 1)

            @of(unit)
            def gather_stats(u):
                r = u % 4
                dve.wait_ge(stats_done, u + 1)
                for t in range(T):
                    last = nc.vector.bn_aggr(mean_var[r][:, t, :], stats[r][:, t, :])
                last.then_inc(mean_var_ready, 1)

            @of(unit)
            def normalize(u):
                r, c = u % 4, u % B
                dve.wait_ge(rstd_ready, u + 1)
                if u >= 4:
                    dve.wait_ge(t_ready, u - 3)
                    if att(u - 4):
                        dve.wait_ge(gram_ps_ready, atts(u - 4))
                for t in range(pooled(u) - pooled(u - 1), first_act_tile(u)):
                    last = nc.vector.tensor_scalar(xn[r][:, t, :], X[:, c, t, :], mean_var[r][:, t, 0:1],
                                                   rstd[r][:, t:t + 1], ALU.subtract, ALU.mult)
                last.then_inc(xn_ready, 1)

            @of(ffn)
            def mix(u):
                n = layers(u)
                dve.wait_ge(mu_x_ready, n)
                prev = bank_T[u % 2][:, 0:S - 1]
                for mixed, m, ready in ((xkT, MU_K, xk_ready), (xrT, MU_R, xr_ready)):
                    rest = mixed[u % 2][:, 1:S]
                    nc.vector.scalar_tensor_tensor(out=rest, in0=prev, scalar=prev_mu[:, m:m + 1], in1=rest,
                                                   op0=ALU.mult, op1=ALU.add).then_inc(ready, 1)

            @of(lambda u: ffn(u) and u != LAST)
            def gate_values(u):
                n = layers(u)
                dve.wait_ge(v_ready, n)
                dve.wait_ge(gate_ready, n)
                if n > 2:
                    dve.wait_ge(x_gated, n - 2)
                nc.vector.scalar_tensor_tensor(out=gated[u % 2][:].rearrange("p t d -> p (t d)"),
                                               in0=gate[u % 2][:].rearrange("p t d -> p (t d)"), scalar=1.0,
                                               in1=bank_V[u % 2][:], op0=ALU.add, op1=ALU.mult).then_inc(gated_ready, 1)

            @of(att)
            def features_k(u):
                n = atts(u)
                dve.wait_ge(ek_ready, n)
                if n > 2:
                    dve.wait_ge(gram_ps_ready, n - 2)
                    dve.wait_ge(kf2_done, n - 2)
                nc.vector.scalar_tensor_tensor(out=kf[u % 2][:], in0=ek[u % 2][:], scalar=1.0, in1=rk[u % 2][:],
                                               op0=ALU.min, op1=ALU.add).then_inc(kf_ready, 1)

            @of(att)
            def features_q(u):
                n = atts(u)
                dve.wait_ge(eq_ready, n)
                nc.vector.scalar_tensor_tensor(out=qfT[u % 2][:], in0=eq[u % 2][:], scalar=1.0, in1=rq[u % 2][:],
                                               op0=ALU.min, op1=ALU.add).then_inc(qf_ready, 1)

            @of(att)
            def spread_ksum(u):
                n = atts(u)
                dve.wait_ge(ksum_ps_ready, n)
                nc.vector.tensor_copy(ksum[u % 2][:], bank_d[:, 0:1])
                nc.vector.tensor_scalar(ksum_head[u % 2][:], head_of[:], bank_d[:, 0:1], None,
                                        ALU.mult).then_inc(ksum_ready, 1)

            @of(att)
            def take_kvo(u):
                n = atts(u)
                dve.wait_ge(kvo_ps_ready, n)
                dve.wait_ge(ksum_ready, n)
                nc.vector.scalar_tensor_tensor(out=kvo[u % 2][:], in0=bv_wo[:], scalar=ksum[u % 2][:],
                                               in1=bank_g[:, 0:D], op0=ALU.mult, op1=ALU.add).then_inc(kvo_ready, 1)

            @of(att)
            def mask_kv(u):
                n = atts(u)
                dve.wait_ge(kvT_ps_ready, n)
                nc.vector.tensor_tensor(kvT[u % 2][:], bank_g[:, 0:D], head_mask[:].rearrange("p h e -> p (h e)"),
                                        ALU.mult).then_inc(kvT_ready, 1)

            @of(att)
            def z_of(u):
                n = atts(u)
                dve.wait_ge(den_ps_ready, n)
                nc.vector.tensor_scalar(den[u % 2][:].rearrange("p t h -> p (t h)"), bank_d[:, 64:64 + T * HEADS],
                                        DEN_EPS, None, ALU.add).then_inc(den_done, 1)
                dve.wait_ge(den_done, n)
                nc.vector.reciprocal(z[u % 2][:], den[u % 2][:]).then_inc(z_ready, 1)

            @of(att)
            def scale_q(u):
                n = atts(u)
                dve.wait_ge(zT_ready, n)
                nc.vector.tensor_tensor(qzT[u % 2][:], qfT[u % 2][:], bank_z[:], ALU.mult).then_inc(qz_ready, 1)

            @of(att)
            def add_attended(u):
                n = atts(u)
                dve.wait_ge(o_ready, n)
                dve.wait_ge(bo_added, n)
                xc = X[:, u % B].rearrange("p t d -> p (t d)")
                nc.vector.tensor_tensor(xc, xc, bank_o[:], ALU.add).then_inc(x_attended, 1)

            def finish_last():
                n, u = layers(LAST), LAST
                dve.wait_ge(gate_ready, n)
                dve.wait_ge(x_gated, n - 2)
                for h in range(2):
                    ts = slice(h * T // 2, (h + 1) * T // 2)
                    cols = slice(h * S // 2, (h + 1) * S // 2)
                    dve.wait_ge(v_ready, n + h)
                    nc.vector.scalar_tensor_tensor(out=gated[u % 2][:, ts, :].rearrange("p t d -> p (t d)"),
                                                   in0=gate[u % 2][:, ts, :].rearrange("p t d -> p (t d)"), scalar=1.0,
                                                   in1=(bank_V[u % 2], bank_V2)[h][:, cols], op0=ALU.add,
                                                   op1=ALU.mult).then_inc(gated_ready, 1)
                    dve.wait_ge(gated_ready, n + h)
                    nc.vector.tensor_tensor(X[:, u % B, ts, :], X[:, u % B, ts, :], gated[u % 2][:, ts, :],
                                            ALU.add).then_inc(last_gated, 1)

            def constants_of_columns():
                dve.wait_ge(columns_loaded, 16)
                nc.vector.tensor_scalar(prev_mu[:], COL[:, 0:2], -1.0, 1.0, ALU.mult, ALU.add).then_inc(setup_done, 1)
                dve.wait_ge(setup_done, 2)
                dve.wait_ge(masks_made, 4)
                nc.vector.tensor_scalar(bv_heads[:], head_mask[:].rearrange("p h e -> p (h e)"), COL[:, BV:BV + 1],
                                        None, ALU.mult).then_inc(setup_done, 1)

            def quarter_of_Wv():
                dve.wait_ge(weights_loaded, 16)
                nc.vector.tensor_scalar(Wv4[:], W[:, W_V, :], 0.25, None, ALU.mult).then_inc(setup_done, 1)

            def stack_bk():
                dve.wait_ge(bias_step, 4)
                for q, p in enumerate((part[0], part[1], part[3])):
                    rows32 = slice(32 * q, 32 * q + 32)
                    nc.vector.tensor_copy(bias_k[rows32], p[rows32])
                nc.vector.memset(bias_k[96:128], 0.0).then_inc(bias_ready, 1)

            def take_bv_wo():
                dve.wait_ge(bv_wo_ps_ready, 1)
                nc.vector.tensor_copy(bv_wo[:], bank[7][:, 0:D]).then_inc(bv_wo_ready, 1)

            stats_of(0)
            gather_stats(0)
            stats_of(1)
            gather_stats(1)
            constants_of_columns()
            normalize(0)
            stats_of(2)
            normalize(1)
            gather_stats(2)
            quarter_of_Wv()
            stats_of(3)
            gather_stats(3)
            mix(0)
            normalize(2)
            stats_of(4)
            gather_stats(4)
            mix(1)
            normalize(3)
            stats_of(5)
            mix(2)
            gather_stats(5)
            stats_of(6)
            stack_bk()
            gather_stats(6)
            normalize(4)
            take_bv_wo()
            gate_values(0)
            for s in range(2, B):
                mix(s + 1)
                normalize(s + 3)
                stats_of(s + 5)
                gate_values(s - 1)
                gather_stats(s + 5)
            for s in range(B, 2 * B):
                stats_of(s + 5)
                scale_q(s - 2)
                mask_kv(s - 1)
                spread_ksum(s - 1)
                features_k(s)
                take_kvo(s - 1)
                gate_values(s - 1)
                gather_stats(s + 5)
                z_of(s - 1)
                mix(s + 1)
                normalize(s + 3)
                add_attended(s - 2)
                features_q(s)
            scale_q(14)
            mask_kv(15)
            spread_ksum(15)
            normalize(19)
            mix(17)
            z_of(15)
            stats_of(21)
            take_kvo(15)
            add_attended(14)
            scale_q(15)
            gate_values(16)
            gather_stats(21)
            mix(18)
            stats_of(22)
            normalize(20)
            add_attended(15)
            for s in range(2 * B + 2, UNITS - 2):
                mix(s + 1)
                gather_stats(s + 4)
                stats_of(s + 5)
                normalize(s + 3)
                gate_values(s - 1)
            mix(23)
            gate_values(21)
            gate_values(22)
            finish_last()

        @block.tensor
        def _(pe):
            @of(unit)
            def transpose_x(u):
                pe.wait_ge(xn_ready, u + 1)
                pe.wait_ge(xn_act_ready, u + 1)
                if pooled(u) > pooled(u - 1):
                    pe.wait_ge(xn_pool_ready, pooled(u))
                if u >= 2:
                    if ffn(u - 2):
                        pe.wait_ge(xr_ready, layers(u - 2))
                    else:
                        pe.wait_ge(xnT_ready, atts(u - 2))
                for t in range(T):
                    last = nc.tensor.transpose(bank_T[u % 2][:, t * P:(t + 1) * P], xn[u % 4][:, t, :], ident[:])
                last.then_inc(t_ready, 1)

            @of(ffn)
            def ffn_k(u):
                n = layers(u)
                pe.wait_ge(xk_ready, n)
                if u == 0:
                    pe.wait_ge(weights_loaded, 16)
                if n > 2:
                    pe.wait_ge(kpos_done, n - 2)
                if u == 2 * B:
                    pe.wait_ge(ek_ready, B)
                if u == 2 * B + 1:
                    pe.wait_ge(kvo_ready, B)
                nc.tensor.matmul(bank_K[u % 2][:], W[:, W_K, :], xkT[u % 2][:], start=True,
                                 stop=True).then_inc(k_ready, 1)

            @of(ffn)
            def ffn_r(u):
                n = layers(u)
                pe.wait_ge(xr_ready, n)
                if n > 2:
                    pe.wait_ge(gate_ready, n - 2)
                if u == 2 * B:
                    pe.wait_ge(eq_ready, B)
                if u == 2 * B + 1:
                    pe.wait_ge(qz_ready, B)
                for t in range(T):
                    last = nc.tensor.matmul(bank_R[u % 2][:, t * P:(t + 1) * P], xrT[u % 2][:, t * P:(t + 1) * P],
                                            W[:, W_R, :], start=True, stop=True)
                last.then_inc(r_ready, 1)

            @of(ffn)
            def ffn_v(u):
                n = layers(u)
                pe.wait_ge(kact_ready, n)
                if n > 2:
                    pe.wait_ge(gated_ready, n - 2)
                if u == 0:
                    pe.wait_ge(setup_done, 4)
                if u == 1:
                    pe.wait_ge(bv_wo_ready, 1)
                if u == 2 * B:
                    pe.wait_ge(den_done, B)
                if u == 2 * B + 1:
                    pe.wait_ge(x_attended, B)
                if u == LAST:
                    pe.wait_ge(kpos_done, n - 1)
                for t in range(T):
                    to = bank_V[u % 2]
                    if u == LAST and t >= T // 2:
                        to = bank_V2
                    last = nc.tensor.matmul(to[:, t * P:(t + 1) * P], kact[u % 2][:, t * P:(t + 1) * P],
                                            Wv4[:], start=True, stop=True)
                    if u == LAST and t == T // 2 - 1:
                        last.then_inc(v_ready, 1)
                last.then_inc(v_ready, 1)

            @of(att)
            def att_k(u):
                n = atts(u)
                pe.wait_ge(xnT_ready, n)
                if n == 1:
                    pe.wait_ge(bias_ready, 1)
                    pe.wait_ge(kpos_done, B - 1)
                if n > 1:
                    pe.wait_ge(ek_ready, n - 1)
                nc.tensor.matmul(bank_k[:], third[:], bias_k[:].unsqueeze(1).to_broadcast([P, T, D]), start=True,
                                 stop=False)
                for t in range(T):
                    last = nc.tensor.matmul(bank_k[:, t * P:(t + 1) * P], xnT[u % 3][:, t * P:(t + 1) * P],
                                            W[:, WK, :], start=False, stop=(t == T - 1))
                last.then_inc(ak_ready, 1)

            @of(att)
            def att_q(u):
                n = atts(u)
                if n == 1:
                    pe.wait_ge(gate_ready, B - 1)
                if n > 1:
                    pe.wait_ge(eq_ready, n - 1)
                nc.tensor.matmul(bank_q[:], W[:, WQ, :], xnT[u % 3][:], start=True, stop=True).then_inc(aq_ready, 1)

            @of(att)
            def att_gram(u):
                n = atts(u)
                pe.wait_ge(kf_ready, n)
                if n == 1:
                    pe.wait_ge(kpos_done, B)
                if n > 1:
                    pe.wait_ge(kvo_ready, n - 1)
                for t in range(T):
                    last = nc.tensor.matmul(bank_g[:, 0:D], xn[u % 4][:, t, :], kf[u % 2][:, t, :],
                                            start=(t == 0), stop=(t == T - 1))
                last.then_inc(gram_ps_ready, 1)

            @of(att)
            def att_ksum(u):
                n = atts(u)
                pe.wait_ge(kf1_ready, n)
                if n == 1:
                    pe.wait_ge(gated_ready, B - 1)
                if n > 1:
                    pe.wait_ge(den_done, n - 1)
                nc.tensor.matmul(bank_d[:, 0:1], kf1[u % 2][:], ones[:], start=True,
                                 stop=True).then_inc(ksum_ps_ready, 1)

            @of(att)
            def att_kv(u):
                n = atts(u)
                pe.wait_ge(gram_ready, n)
                nc.tensor.matmul(bank_g[:, 0:D], W[:, WV, :], gram[u % 2][:], start=True,
                                 stop=True).then_inc(kvT_ps_ready, 1)

            @of(att)
            def att_den(u):
                n = atts(u)
                pe.wait_ge(qf_ready, n)
                pe.wait_ge(ksum_ready, n)
                for t in range(T):
                    last = nc.tensor.matmul(bank_d[:, 64 + t * HEADS:64 + (t + 1) * HEADS],
                                            qfT[u % 2][:, t * P:(t + 1) * P], ksum_head[u % 2][:], start=True,
                                            stop=True)
                last.then_inc(den_ps_ready, 1)

            @of(att)
            def att_z(u):
                n = atts(u)
                pe.wait_ge(z_wide_ready, n)
                if n == 1:
                    pe.wait_ge(gate_ready, B)
                if n > 1:
                    pe.wait_ge(qz_ready, n - 1)
                for t in range(T):
                    last = nc.tensor.transpose(bank_z[:, t * P:(t + 1) * P],
                                               z_wide[u % 2][:, t].rearrange("p h e -> p (h e)"), ident[:])
                last.then_inc(zT_ready, 1)

            @of(att)
            def att_kvo(u):
                n = atts(u)
                pe.wait_ge(kvT_ready, n)
                nc.tensor.matmul(bank_g[:, 0:D], kvT[u % 2][:], W[:, WO, :], start=True,
                                 stop=True).then_inc(kvo_ps_ready, 1)

            @of(att)
            def att_out(u):
                n = atts(u)
                pe.wait_ge(kvo_ready, n)
                pe.wait_ge(qz_ready, n)
                if n == 1:
                    pe.wait_ge(gated_ready, B)
                if n > 1:
                    pe.wait_ge(x_attended, n - 1)
                for t in range(T):
                    last = nc.tensor.matmul(bank_o[:, t * P:(t + 1) * P], qzT[u % 2][:, t * P:(t + 1) * P],
                                            kvo[u % 2][:], start=True, stop=True)
                last.then_inc(o_ready, 1)

            def keep_warm(n):
                for _ in range(n):
                    nc.tensor.matmul(bank[7][:, 0:P], third[:], third[:], start=True, stop=True)

            def bv_by_wo():
                pe.wait_ge(setup_done, 3)
                pe.wait_ge(weights_loaded, 16)
                nc.tensor.matmul(bank[7][:, 0:D], bv_heads[:], W[:, WO, :], start=True,
                                 stop=True).then_inc(bv_wo_ps_ready, 1)

            pe.wait_ge(setup_done, 1)
            keep_warm(50)
            pe.wait_ge(id_made, 1)
            transpose_x(0)
            keep_warm(15)
            keep_warm(10)
            transpose_x(1)
            ffn_k(0)
            ffn_r(0)
            transpose_x(2)
            ffn_k(1)
            ffn_r(1)
            transpose_x(3)
            bv_by_wo()
            ffn_v(0)
            for s in range(2, B):
                ffn_k(s)
                ffn_r(s)
                transpose_x(s + 2)
                ffn_v(s - 1)
            for s in range(B, 2 * B):
                att_k(s)
                att_kv(s - 1)
                att_ksum(s - 1)
                att_q(s)
                ffn_v(s - 1)
                att_kvo(s - 1)
                att_den(s - 1)
                transpose_x(s + 2)
                att_out(s - 2)
                att_gram(s)
                att_z(s - 1)
            att_ksum(15)
            ffn_k(16)
            att_kv(15)
            ffn_r(16)
            att_kvo(15)
            att_den(15)
            att_out(14)
            transpose_x(18)
            ffn_v(16)
            att_z(15)
            ffn_k(17)
            transpose_x(19)
            ffn_r(17)
            att_out(15)
            for s in range(2 * B + 2, UNITS - 2):
                ffn_k(s)
                ffn_r(s)
                transpose_x(s + 2)
                ffn_v(s - 1)
            ffn_k(22)
            ffn_r(22)
            ffn_v(21)
            ffn_k(23)
            ffn_v(22)
            ffn_r(23)
            ffn_v(23)


def kernel(**inputs):
    import concourse.bacc as bacc
    from concourse.bass_utils import run_bass_kernel_spmd as run

    given = {k: np.ascontiguousarray(v) for k, v in inputs.items()}
    arrays = {
        "x": given["L0_attn_x"],
        "weights": np.concatenate([given[f"L0_ffn_{n}"].T for n in ("W_r", "W_k", "W_v")]
                                  + [given[f"L0_attn_{n}"] for n in ("wq", "wk", "wv", "wo")], axis=0),
        "columns": np.stack([given["L0_ffn_mu_r"], given["L0_ffn_mu_k"], given["L0_attn_bq"], given["L0_attn_bv"]],
                            axis=1),
        "rows": np.stack([given["L0_attn_bk"], given["L0_attn_bo"]], axis=0),
    }
    arrays = {k: np.ascontiguousarray(v) for k, v in arrays.items()}
    nc = bacc.Bacc("TRN2", target_bir_lowering=False, num_devices=1)
    args = [nc.dram_tensor(k, v.shape, mybir.dt.from_np(v.dtype), kind="ExternalInput").ap() for k, v in arrays.items()]
    out = nc.dram_tensor("out", arrays["x"].shape, mybir.dt.float32, kind="ExternalOutput").ap()
    macaron_block(nc, *args, out)
    r = run(nc, [arrays], core_ids=[0])
    return r.results[0]["out"]
```
